# Optimizing a Trainium2 kernel written in Bass

```python
import numpy as np
import jax
import jax.numpy as jnp

def _softmax(x, axis=-1):
    return jax.nn.softmax(x, axis=axis)

def _gelu(x):
    return jax.nn.gelu(x, approximate=True)

def _silu(x):
    return jax.nn.silu(x)

def _sigmoid(x):
    return jax.nn.sigmoid(x)

def _layernorm(x, axis=-1, eps=1e-05):
    m = jnp.mean(x, axis=axis, keepdims=True)
    v = jnp.var(x, axis=axis, keepdims=True)
    return (x - m) / jnp.sqrt(v + eps)

def _scatter_add(tgt, idx, src, axis=0):
    return tgt.at[idx].add(src)

def _segment_sum(src, seg, n):
    return jax.ops.segment_sum(src, seg, n)
kernel_name = 'mk_cond_seq_d4_seqx_r8_cc47ad'

def setup_inputs(seed: int=0):
    np.random.seed(seed)
    _w = jnp.asarray

    def _rec_inputs():
        import jax
        import jax.numpy as jnp
        _rk = jax.random.key(seed)
        x = -1.528e-05 + 0.9999 * jax.random.normal(jax.random.fold_in(_rk, 1), (4, 256, 256), jnp.float32)
        _lenS = 256 - jax.random.randint(jax.random.fold_in(_rk, 7), (4,), 0, max(1, 256 // 4) + 1, jnp.int32)
        _lenS2 = 256 - jax.random.randint(jax.random.fold_in(_rk, 8), (4,), 0, max(1, 256 // 4) + 1, jnp.int32)
        itok_B_1_2 = jax.random.randint(jax.random.fold_in(_rk, 11), (4,), 1, 3, jnp.int32)
        itok_B_17_1546 = jax.random.randint(jax.random.fold_in(_rk, 13), (4,), 17, 1547, jnp.int32)
        return (x, itok_B_1_2, itok_B_17_1546, _lenS)
    x, itok_B_1_2, itok_B_17_1546, _lenS = _rec_inputs()

    def _L0_cond_setup():
        import jax, jax.numpy as jnp
        import numpy as np
        H = 256
        K = 128
        R = 3
        B = 8
        S = 256
        LN_EPS = 1e-05
        key = jax.random.key(seed)
        ks = jax.random.split(key, 8)
        sd_d = 1.0 / np.sqrt(H)
        sd_u = 1.0 / np.sqrt(K)
        return {'role': jax.random.randint(ks[0], (B,), 0, R), 'hidden_states': jax.random.normal(ks[1], (B, S, H), dtype=jnp.float32), 'W_down': jax.random.uniform(ks[2], (R, H, K), jnp.float32, -sd_d, sd_d), 'b_down': jax.random.uniform(ks[3], (R, K), jnp.float32, -sd_d, sd_d), 'W_up': jax.random.uniform(ks[4], (R, K, H), jnp.float32, -sd_u, sd_u), 'b_up': jax.random.uniform(ks[5], (R, H), jnp.float32, -sd_u, sd_u), 'gamma': jnp.ones((R, H), jnp.float32), 'beta': jnp.zeros((R, H), jnp.float32)}
    _L0_cond_all = _L0_cond_setup()
    _L0_cond_in = {k: v for k, v in _L0_cond_all.items() if k in ('W_down', 'b_down', 'W_up', 'b_up', 'gamma', 'beta')}
    del _L0_cond_all

    def _L1_cond_setup():
        import jax, jax.numpy as jnp
        import numpy as np
        B, T, V = (8, 64, 256)
        H = 4 * V
        key = jax.random.key(seed)
        ks = jax.random.split(key, 16)
        s = lambda n: 1.0 / np.sqrt(n)
        inp = {'x': jax.random.uniform(ks[0], (B, T, V), dtype=jnp.float32), 'lens': jax.random.randint(ks[1], (B,), 1, T, dtype=jnp.int64), 'target_codes': jax.random.randint(ks[2], (B,), 0, V, dtype=jnp.int64), 'Wq': jax.random.normal(ks[3], (V, V), jnp.float32) * s(V), 'Wk': jax.random.normal(ks[4], (V, V), jnp.float32) * s(V), 'Wv': jax.random.normal(ks[5], (V, V), jnp.float32) * s(V), 'Wp': jax.random.normal(ks[6], (V, V), jnp.float32) * s(V), 'bp': jnp.zeros((V,), jnp.float32), 'cW1': jax.random.normal(ks[7], (V, H), jnp.float32) * s(V), 'cb1': jnp.zeros((H,), jnp.float32), 'cW2': jax.random.normal(ks[8], (H, V), jnp.float32) * s(H), 'cb2': jnp.zeros((V,), jnp.float32), 'mW1': jax.random.normal(ks[9], (2 * V, H), jnp.float32) * s(2 * V), 'mb1': jnp.zeros((H,), jnp.float32), 'mW2': jax.random.normal(ks[10], (H, V), jnp.float32) * s(H), 'mb2': jnp.zeros((V,), jnp.float32)}
        return inp
    _L1_cond_all = _L1_cond_setup()
    _L1_cond_in = {k: v for k, v in _L1_cond_all.items() if k in ('Wq', 'Wk', 'Wv', 'Wp', 'bp', 'cW1', 'cb1', 'cW2', 'cb2', 'mW1', 'mb1', 'mW2', 'mb2')}
    del _L1_cond_all

    def _L2_cond_setup():
        import jax, jax.numpy as jnp
        import numpy as np
        B, S, H = (8, 256, 256)
        BN = 128
        E = 3
        LN_EPS = 1e-05
        key = jax.random.key(seed)
        ks = jax.random.split(key, 8)
        stream = jax.random.randint(ks[0], (B,), 0, E, dtype=jnp.int32)
        hidden_states = jax.random.normal(ks[1], (B, S, H), dtype=jnp.float32)
        W_down = jax.random.normal(ks[2], (E, H, BN), dtype=jnp.float32) * 0.02
        b_down = jnp.zeros((E, BN), dtype=jnp.float32)
        W_up = jax.random.normal(ks[3], (E, BN, H), dtype=jnp.float32) * 0.02
        b_up = jnp.zeros((E, H), dtype=jnp.float32)
        ln_w = jnp.ones((E, H), dtype=jnp.float32)
        ln_b = jnp.zeros((E, H), dtype=jnp.float32)
        return {'stream': stream, 'hidden_states': hidden_states, 'W_down': W_down, 'b_down': b_down, 'W_up': W_up, 'b_up': b_up, 'ln_w': ln_w, 'ln_b': ln_b}
    _L2_cond_all = _L2_cond_setup()
    _L2_cond_in = {k: v for k, v in _L2_cond_all.items() if k in ('W_down', 'b_down', 'W_up', 'b_up', 'ln_w', 'ln_b')}
    del _L2_cond_all

    def _L3_cond_setup():
        import jax, jax.numpy as jnp
        import numpy as np
        H = 256
        K = 128
        R = 3
        B = 8
        S = 256
        LN_EPS = 1e-05
        key = jax.random.key(seed)
        ks = jax.random.split(key, 8)
        sd_d = 1.0 / np.sqrt(H)
        sd_u = 1.0 / np.sqrt(K)
        return {'role': jax.random.randint(ks[0], (B,), 0, R), 'hidden_states': jax.random.normal(ks[1], (B, S, H), dtype=jnp.float32), 'W_down': jax.random.uniform(ks[2], (R, H, K), jnp.float32, -sd_d, sd_d), 'b_down': jax.random.uniform(ks[3], (R, K), jnp.float32, -sd_d, sd_d), 'W_up': jax.random.uniform(ks[4], (R, K, H), jnp.float32, -sd_u, sd_u), 'b_up': jax.random.uniform(ks[5], (R, H), jnp.float32, -sd_u, sd_u), 'gamma': jnp.ones((R, H), jnp.float32), 'beta': jnp.zeros((R, H), jnp.float32)}
    _L3_cond_all = _L3_cond_setup()
    _L3_cond_in = {k: v for k, v in _L3_cond_all.items() if k in ('W_down', 'b_down', 'W_up', 'b_up', 'gamma', 'beta')}
    del _L3_cond_all
    return {'x': x, 'itok_B_1_2': itok_B_1_2, 'itok_B_17_1546': itok_B_17_1546, '_lenS': _lenS, 'L0_cond_W_down': _L0_cond_in['W_down'], 'L0_cond_b_down': _L0_cond_in['b_down'], 'L0_cond_W_up': _L0_cond_in['W_up'], 'L0_cond_b_up': _L0_cond_in['b_up'], 'L0_cond_gamma': _L0_cond_in['gamma'], 'L0_cond_beta': _L0_cond_in['beta'], 'L1_cond_Wq': _L1_cond_in['Wq'], 'L1_cond_Wk': _L1_cond_in['Wk'], 'L1_cond_Wv': _L1_cond_in['Wv'], 'L1_cond_Wp': _L1_cond_in['Wp'], 'L1_cond_bp': _L1_cond_in['bp'], 'L1_cond_cW1': _L1_cond_in['cW1'], 'L1_cond_cb1': _L1_cond_in['cb1'], 'L1_cond_cW2': _L1_cond_in['cW2'], 'L1_cond_cb2': _L1_cond_in['cb2'], 'L1_cond_mW1': _L1_cond_in['mW1'], 'L1_cond_mb1': _L1_cond_in['mb1'], 'L1_cond_mW2': _L1_cond_in['mW2'], 'L1_cond_mb2': _L1_cond_in['mb2'], 'L2_cond_W_down': _L2_cond_in['W_down'], 'L2_cond_b_down': _L2_cond_in['b_down'], 'L2_cond_W_up': _L2_cond_in['W_up'], 'L2_cond_b_up': _L2_cond_in['b_up'], 'L2_cond_ln_w': _L2_cond_in['ln_w'], 'L2_cond_ln_b': _L2_cond_in['ln_b'], 'L3_cond_W_down': _L3_cond_in['W_down'], 'L3_cond_b_down': _L3_cond_in['b_down'], 'L3_cond_W_up': _L3_cond_in['W_up'], 'L3_cond_b_up': _L3_cond_in['b_up'], 'L3_cond_gamma': _L3_cond_in['gamma'], 'L3_cond_beta': _L3_cond_in['beta']}

def reference(x, itok_B_1_2, itok_B_17_1546, _lenS, L0_cond_W_down, L0_cond_b_down, L0_cond_W_up, L0_cond_b_up, L0_cond_gamma, L0_cond_beta, L1_cond_Wq, L1_cond_Wk, L1_cond_Wv, L1_cond_Wp, L1_cond_bp, L1_cond_cW1, L1_cond_cb1, L1_cond_cW2, L1_cond_cb2, L1_cond_mW1, L1_cond_mb1, L1_cond_mW2, L1_cond_mb2, L2_cond_W_down, L2_cond_b_down, L2_cond_W_up, L2_cond_b_up, L2_cond_ln_w, L2_cond_ln_b, L3_cond_W_down, L3_cond_b_down, L3_cond_W_up, L3_cond_b_up, L3_cond_gamma, L3_cond_beta):
    import jax
    import jax.numpy as jnp

    def _L0_cond_ref(role, hidden_states, W_down, b_down, W_up, b_up, gamma, beta):
        import jax, jax.numpy as jnp
        import numpy as np
        H = 256
        K = 128
        R = 3
        B = 8
        S = 256
        LN_EPS = 1e-05
        h = jnp.einsum('bsh,bhk->bsk', hidden_states, W_down[role]) + b_down[role][:, None, :]
        h = jax.nn.gelu(h, approximate=False)
        u = jnp.einsum('bsk,bkh->bsh', h, W_up[role]) + b_up[role][:, None, :]
        y = hidden_states + u
        mean = jnp.mean(y, axis=-1, keepdims=True)
        var = jnp.mean(jnp.square(y - mean), axis=-1, keepdims=True)
        yn = (y - mean) * jax.lax.rsqrt(var + LN_EPS)
        return yn * gamma[role][:, None, :] + beta[role][:, None, :]

    def _L1_cond_ref(x, lens, target_codes, Wq, Wk, Wv, Wp, bp, cW1, cb1, cW2, cb2, mW1, mb1, mW2, mb2):
        import jax, jax.numpy as jnp
        import numpy as np
        B, T, V = (8, 64, 256)
        H = 4 * V
        scale = V ** (-0.5)
        q = x @ Wq
        k = x @ Wk
        v = x @ Wv
        attn = jnp.einsum('btd,bTd->btT', q, k) * scale
        attn = jax.nn.softmax(attn, axis=-1)
        attn_out = jnp.einsum('btT,bTd->btd', attn, v) @ Wp + bp
        target_embed = jax.nn.one_hot(target_codes, V, dtype=x.dtype)[:, None, :]
        cms_out = jax.nn.gelu(attn_out @ cW1 + cb1, approximate=False) @ cW2 + cb2
        cms_out = cms_out + target_embed
        concat = jnp.concatenate([attn_out, cms_out], axis=-1)
        modifier = jax.nn.gelu(concat @ mW1 + mb1, approximate=False) @ mW2 + mb2
        out = jnp.clip(x + cms_out + modifier, 0.0, 1.0)
        return out

    def _L2_cond_ref(stream, hidden_states, W_down, b_down, W_up, b_up, ln_w, ln_b):
        import jax, jax.numpy as jnp
        import numpy as np
        B, S, H = (8, 256, 256)
        BN = 128
        E = 3
        LN_EPS = 1e-05
        Wd = W_down[stream]
        bd = b_down[stream]
        Wu = W_up[stream]
        bu = b_up[stream]
        g = ln_w[stream]
        b = ln_b[stream]
        residual = hidden_states
        h = jnp.einsum('bsh,bhk->bsk', hidden_states, Wd) + bd[:, None, :]
        h = jax.nn.gelu(h, approximate=False)
        h = jnp.einsum('bsk,bkh->bsh', h, Wu) + bu[:, None, :]
        h = residual + h
        mean = jnp.mean(h, axis=-1, keepdims=True)
        var = jnp.mean(jnp.square(h - mean), axis=-1, keepdims=True)
        h = (h - mean) * jax.lax.rsqrt(var + LN_EPS)
        return h * g[:, None, :] + b[:, None, :]

    def _L3_cond_ref(role, hidden_states, W_down, b_down, W_up, b_up, gamma, beta):
        import jax, jax.numpy as jnp
        import numpy as np
        H = 256
        K = 128
        R = 3
        B = 8
        S = 256
        LN_EPS = 1e-05
        h = jnp.einsum('bsh,bhk->bsk', hidden_states, W_down[role]) + b_down[role][:, None, :]
        h = jax.nn.gelu(h, approximate=False)
        u = jnp.einsum('bsk,bkh->bsh', h, W_up[role]) + b_up[role][:, None, :]
        y = hidden_states + u
        mean = jnp.mean(y, axis=-1, keepdims=True)
        var = jnp.mean(jnp.square(y - mean), axis=-1, keepdims=True)
        yn = (y - mean) * jax.lax.rsqrt(var + LN_EPS)
        return yn * gamma[role][:, None, :] + beta[role][:, None, :]
    x = _L0_cond_ref(itok_B_1_2, x, L0_cond_W_down, L0_cond_b_down, L0_cond_W_up, L0_cond_b_up, L0_cond_gamma, L0_cond_beta)
    x = _L1_cond_ref(x, _lenS, itok_B_17_1546, L1_cond_Wq, L1_cond_Wk, L1_cond_Wv, L1_cond_Wp, L1_cond_bp, L1_cond_cW1, L1_cond_cb1, L1_cond_cW2, L1_cond_cb2, L1_cond_mW1, L1_cond_mb1, L1_cond_mW2, L1_cond_mb2)
    x = _L2_cond_ref(itok_B_1_2, x, L2_cond_W_down, L2_cond_b_down, L2_cond_W_up, L2_cond_b_up, L2_cond_ln_w, L2_cond_ln_b)
    x = _L3_cond_ref(itok_B_1_2, x, L3_cond_W_down, L3_cond_b_down, L3_cond_W_up, L3_cond_b_up, L3_cond_gamma, L3_cond_beta)
    return x

_drawn_inputs = setup_inputs


def setup_inputs(seed=0):
    import zlib

    import numpy as np

    out = dict(_drawn_inputs(seed))
    spreads = {'L0_cond_gamma': (1.0, 0.2),
     'L0_cond_beta': (0.0, 0.1),
     'L1_cond_bp': (0.0, 0.1),
     'L1_cond_cb1': (0.0, 0.1),
     'L1_cond_cb2': (0.0, 0.1),
     'L1_cond_mb1': (0.0, 0.1),
     'L1_cond_mb2': (0.0, 0.1),
     'L2_cond_b_down': (0.0, 0.301),
     'L2_cond_b_up': (0.0, 0.1),
     'L2_cond_ln_w': (1.0, 0.2),
     'L2_cond_ln_b': (0.0, 0.1),
     'L3_cond_gamma': (1.0, 0.2),
     'L3_cond_beta': (0.0, 0.1)}
    factors = {'L0_cond_b_down': 3.157, 'L3_cond_b_down': 5.374}
    for name, (base, spread) in spreads.items():
        noise = np.random.default_rng([zlib.crc32(name.encode()), seed]).standard_normal(out[name].shape)
        drawn = base * np.exp(spread * noise) if base else spread * noise
        out[name] = jnp.asarray(drawn.astype(out[name].dtype))
    for name, factor in factors.items():
        out[name] = (out[name] * factor).astype(out[name].dtype)
    return out
```

```python
from contextlib import ExitStack

import concourse.bass as bass
from concourse import mybir

P = 128
F32 = mybir.dt.float32
F32R = mybir.dt.float32r
I32 = mybir.dt.int32
ALU = mybir.AluOpType
ACT = mybir.ActivationFunctionType
AX_X = mybir.AxisListType.X

B, S, V = 4, 256, 256
KF = V // P
TT = S // P
CB = 2
NC = B // CB
CT = CB * S
HT = 4 * V // P
E = 3
LN_EPS = 1e-5
HI, LO = 0, 1
PASSES = ((HI, HI), (HI, LO), (LO, HI))
PIECE = 512
RAW_SLOTS = 6
ADP_SLOTS = 4
HID_SLOTS = 3
RING = 6
LAYERS = (0, 2, 3)

BD = {0: 0, 2: 5, 3: 10}
GAMMA = {0: 1, 2: 6}
BETA = {0: 3, 2: 8}
EV = 11
CB1, MB1, BP, CB2, MB2 = 0, HT, 2 * HT, 2 * HT + KF, 2 * HT + 2 * KF
SV = 2 * HT + 3 * KF


def splitter(piece):
    kind, i = piece
    if kind == "x" or (kind == "adp" and i[0] == 0) or (kind == "mn" and i < 2):
        return "AV"
    return "P"


def order():
    o = []

    def split(kind, i):
        o.append(("W", (kind, i)))

    for b in range(2):
        split("x", b)
        split("adp", (0, b))
        o.append(("D", (0, b)))
    split("mn", 2)
    split("mn", 3)
    chain = [("D",), ("U",), ("N",), ("MN",), ("T",), ("Y",), ("S", "E", "V"), ("PT",), ("A",)]
    weights = iter(range(20))
    done = {("D", 0), ("D", 1)}
    for step in range(B + len(chain)):
        for k in reversed(range(len(chain))):
            b = step - k
            if not 0 <= b < B:
                continue
            for kind in chain[k]:
                if (kind, b) in done:
                    continue
                if kind == "MN":
                    if b < 2:
                        o.append(("MN", b))
                    continue
                if kind == "D":
                    split("x", b)
                    split("adp", (0, b))
                    if b == 2:
                        split("mn", 0)
                        split("mn", 1)
                o.append((kind, (0, b) if kind in "DUNT" else b))
        if step >= 1:
            for i in range(2 if step < 9 else 1):
                n = next(weights, None)
                if n is not None:
                    split("w", n)

    late = [("W", ("w", n)) for n in weights]
    adapters = [("W", ("adp", (l, b))) for c in range(NC) for b in range(CB * c, CB * c + CB) for l in (2, 3)]

    def tail(bs):
        seq = [("D", 2), ("U", 2), ("N", 2), ("T", 2), ("D", 3), ("U", 3), ("F", 3)]
        out = []
        for step in range(len(seq) + len(bs) - 1):
            for k in reversed(range(len(seq))):
                if 0 <= step - k < len(bs):
                    out.append((seq[k][0], (seq[k][1], bs[step - k])))
        return out

    for c in range(NC):
        fill = late + adapters[:4] if c == 0 else []
        work = tail(range(0, CB)) if c == 1 else []
        mlp = []
        for ht in range(HT):
            mlp.append([("H1", (c, ht))] + ([("CMS", (c, ht - 1))] if ht else []))
        mlp.append([("CMS", (c, HT - 1)), ("CE", c)])
        mlp.append([("H2A", (c, 0)), ("H2A", (c, 1)), ("H2A", (c, 2)), ("H2B", (c, 0))])
        for ht in range(1, HT):
            nxt = [("H2A", (c, ht + 2))] if ht + 2 < HT else []
            mlp.append([("H2B", (c, ht)), ("MOD", (c, ht - 1))] + nxt)
        mlp.append([("MOD", (c, HT - 1))] + [("ME", b) for b in range(CB * c, CB * c + CB)])
        per = -(-len(work) // (len(mlp) - 3)) if work else 0
        for i, group in enumerate(mlp):
            o.extend(group)
            for _ in range(2):
                if fill:
                    o.append(fill.pop(0))
            if i >= 1 and work:
                o.extend(work[:per])
                del work[:per]
            if c == 1 and 9 <= i and adapters[4:]:
                o.append(adapters.pop(4))
        o.extend(fill + work)
        if c == 0:
            adapters = adapters
    o.extend(adapters[4:])
    o.extend(tail(range(CB, B)))
    assert len(set(o)) == len(o)
    return o


def build(nc, roles, codes, xs, weights, adapters, expert_vecs, expert_rows, vecs, out):
    ORDER = order()
    PIECES = [(*i, splitter(i)) for kind, i in ORDER if kind == "W"]
    nth_of, seen = {}, {}
    for kind, i in ORDER:
        seen[kind] = seen.get(kind, 0) + 1
        nth_of[(kind, i)] = seen[kind]

    def nth(kind, i):
        return nth_of[(kind, i)]

    bank_of, before = {}, {}
    last, n = [None] * RING, 0
    for kind, i in ORDER:
        if kind in ("D", "U", "T", "MN", "Y", "V", "S", "PT", "A", "H1", "H2A"):
            bank_of[(kind, i)] = n % RING
            before[(kind, i)] = last[n % RING]
            last[n % RING] = (kind, i)
            n += 1

    def hid(phase, c, ht):
        return (c * 2 + phase) * HT + ht

    slot_of, split_count, prev_in_slot = {}, {}, {}
    users = [None] * RAW_SLOTS
    counts = {"AV": 0, "P": 0}
    for n, (kind, i, who) in enumerate(PIECES):
        slot_of[(kind, i)] = n % RAW_SLOTS
        prev_in_slot[(kind, i)] = users[n % RAW_SLOTS]
        users[n % RAW_SLOTS] = (kind, i)
    who_of = {(k, i): w for k, i, w in PIECES}
    for kind, i in ORDER:
        if kind == "W":
            counts[who_of[i]] += 1
            split_count[i] = counts[who_of[i]]
    use_of_slot = {}
    for n, (kind, i, _) in enumerate(PIECES):
        use_of_slot[(kind, i)] = n // RAW_SLOTS + 1
    adp_pieces = [i for k, i, _ in PIECES if k == "adp"]
    adp_slot = {i: n % ADP_SLOTS for n, i in enumerate(adp_pieces)}
    adp_before = {i: (adp_pieces[n - ADP_SLOTS] if n >= ADP_SLOTS else None) for n, i in enumerate(adp_pieces)}

    with ExitStack() as ctx:
        def sb(name, shape, dt=F32):
            return ctx.enter_context(nc.sbuf_tensor(name, shape, dt))

        def sem(name):
            return ctx.enter_context(nc.semaphore(name))

        raw = sb("raw", [P, RAW_SLOTS, PIECE])
        w1 = sb("w1", [P, 2, HT, KF, P], F32R)
        w2 = sb("w2", [P, 2, HT, V], F32R)
        w3 = sb("w3", [P, 2, HT, 2 * KF, P], F32R)
        w4 = sb("w4", [P, 2, HT, V], F32R)
        adp = sb("adp", [P, 2, ADP_SLOTS, PIECE], F32R)
        mn = sb("mn", [P, 2, 2, KF, V], F32R)
        xin = sb("xin", [P, 2, 2, KF, S], F32R)
        xmid = sb("xmid", [P, 2, 2, KF, S], F32R)
        res = sb("res", [P, B, KF, S])
        qk = sb("qk", [P, 2, KF, S], F32R)
        vv = sb("vv", [P, 2, 2, TT, V], F32R)
        prob = sb("prob", [P, TT, S])
        probT = sb("probT", [P, 2, TT, S], F32R)
        attn = sb("attn", [P, NC, 2, KF, CT], F32R)
        hidden = sb("hidden", [P, HID_SLOTS, 2, CT], F32R)
        hidden_full = sb("hidden_full", [P, 2, CT])
        cms = sb("cms", [P, 2, KF, CT], F32R)
        act_h = sb("act_h", [P, 2, 2, S], F32R)
        act_full = sb("act_full", [P, S])
        yn = sb("yn", [P, 2, TT, V])
        full = sb("full", [P, KF, S])
        gb = sb("gb", [P, 2, 2, V])
        rows = sb("rows", [P, 2, 3, V], F32R)
        ones_row = sb("ones_row", [P, B, P], F32R)
        ident_r = sb("ident_r", [P, P], F32R)
        ident = ident_r[:, :].bitcast(F32)
        ev = sb("ev", [P, B, EV])
        sv = sb("sv", [P, SV])
        code_i = sb("code_i", [P, B], I32)
        code_f = sb("code_f", [P, B])
        feat_i = sb("feat_i", [P, KF], I32)
        feat_f = sb("feat_f", [P, KF])
        cbias = sb("cbias", [P, KF, B])
        rbias = sb("rbias", [P, KF, B])
        bn = sb("bn", [P, B, TT, 6])
        mv = sb("mv", [P, 3, B, TT, 2])
        veps = sb("veps", [P, 3, B, TT])
        rstd = sb("rstd", [P, 3, B, TT])
        nmr = sb("nmr", [P, 3, B, TT])
        mhalf = sb("mhalf", [P, TT])
        smax = sb("smax", [P, B, TT])
        nmax = sb("nmax", [P, B, TT])
        ssum = sb("ssum", [P, B, TT])
        rsum = sb("rsum", [P, B, TT])

        ring = [ctx.enter_context(nc.psum_tensor(f"ring{i}", [P, 512], F32)) for i in range(RING)]
        acc = ctx.enter_context(nc.psum_tensor("acc", [P, KF, CT], F32))

        def bank(kind, i, two=2):
            return ring[bank_of[(kind, i)]][:, :].rearrange("p (a b) -> p a b", a=two)

        s_raw = [sem(f"raw_landed{i}") for i in range(RAW_SLOTS)]
        s_vec, s_code, s_rows = sem("vecs_landed"), sem("codes_landed"), sem("rows_landed")
        s_ev = sem("expert_vecs_landed")
        s_gb = [sem(f"gamma_beta_landed{i}") for i in range(2)]
        s_out = sem("out_landed")
        act_w, dve_w, pool_hi, pool_w = sem("act_W_hi"), sem("dve_W_lo"), sem("pool_W_hi"), sem("pool_W_lo")
        pool_zero, pool_const = sem("pool_zeros"), sem("pool_constants")
        dve_const, dve_rows, dve_link = sem("dve_constants"), sem("dve_rows"), sem("dve_link")
        pe = {k: sem(f"pe_{k}") for k in ("D", "U", "T", "MN", "Y", "V", "S", "PT", "A", "hidden", "hidden_used")}
        act = {k: sem(f"act_{k}") for k in ("D", "N", "T", "MN", "Y", "V", "E", "PT", "A", "hidden", "CE")}
        dve = {k: sem(f"dve_{k}") for k in
               ("D", "U", "N", "T", "MN", "Y", "V", "max", "E", "PT", "A", "hidden", "CE", "z", "ME", "F")}
        pool_rstd = sem("pool_rstd")
        pool_eps = sem("pool_link")

        def freed(step):
            kind, i = step
            k = nth(kind, i)
            if kind == "D":
                return [(act["D"], 2 * k)]
            if kind == "U":
                if i[0] == 3:
                    return [(dve["F"], 2 * nth("F", i))]
                return [(act["N"], TT * nth("N", i))]
            if kind == "T":
                return [(act["T"], KF * k)]
            if kind == "S":
                return [(act["E"], TT * k)]
            if kind in ("MN", "Y", "V", "PT"):
                return [(dve[kind], k)]
            if kind == "A":
                return [(dve["A"], KF * k)]
            m = hid(0 if kind == "H1" else 1, *i)
            return [(act["hidden"], 2 * (m + 1))]

        def split_done(piece):
            return (dve_w if who_of[piece] == "AV" else pool_w), split_count[piece]

        def split_target(piece, part):
            kind, i = piece
            if kind == "x":
                return xin[:, part, i % 2, :, :].rearrange("p a b -> p (a b)")
            if kind == "adp":
                return adp[:, part, adp_slot[i], :]
            if kind == "mn":
                return w4[:, part, 2 * i:2 * i + 2, :].rearrange("p a b -> p (a b)")
            if i < 4:
                return w1[:, part, 2 * i:2 * i + 2, :, :].rearrange("p a b c -> p (a b c)")
            if i < 8:
                return w2[:, part, 2 * (i - 4):2 * (i - 4) + 2, :].rearrange("p a b -> p (a b)")
            if i < 16:
                return w3[:, part, i - 8, :, :].rearrange("p a b -> p (a b)")
            return w4[:, part, 2 * (i - 16):2 * (i - 16) + 2, :].rearrange("p a b -> p (a b)")

        def target_free(piece):
            kind, i = piece
            if kind == "x" and i >= 2:
                return [(pe["U"], nth("U", (0, i - 2)))]
            if kind == "adp" and adp_before[i]:
                return [(pe["U"], nth("U", adp_before[i]))]
            if kind == "w" and i >= 16:
                return [(pe["MN"], 2)]
            return []

        def layer_in(l, b, part):
            return (xmid if l == 3 else xin)[:, part, b % 2]

        def attn_of(b, part, kf):
            return attn[:, b // CB, part, kf, (b % CB) * S:(b % CB + 1) * S]

        def pair(kind, i, part):
            return {"MN": mn[:, part, i % 2], "Y": qk[:, part], "V": vv[:, part, i % 2],
                    "PT": probT[:, part]}[kind]

        def layer_out(l, b):
            return res[:, b] if l == 0 else full

        li = {l: n for n, l in enumerate(LAYERS)}
        block = ctx.enter_context(nc.Block())

        @block.sync
        def _(sp):
            role = [sp.value_load(roles[0:1, b:b + 1], min_val=0, max_val=E - 1) for b in range(B)]

            def load(kind, i):
                slot = slot_of[(kind, i)]
                if prev_in_slot[(kind, i)]:
                    sp.wait_ge(*split_done(prev_in_slot[(kind, i)]))
                if kind == "adp":
                    src = adapters[bass.ds(role[i[1]] + E * li[i[0]], 1), :, :].rearrange("o p n -> p (o n)")
                else:
                    src = weights[{"mn": 0, "w": 4}[kind] + i, :, :]
                sp.dma_start(raw[:, slot, :], src).then_inc(s_raw[slot], 16)

            def gamma_beta(b):
                if b >= 2:
                    sp.wait_ge(dve["F"], 2 * nth("F", (3, b - 2)))
                sp.dma_start(gb[:, b % 2, :, :].rearrange("p a v -> p (a v)"),
                             expert_rows[bass.ds(role[b], 1), 3 * V:5 * V].partition_broadcast(P)
                             .rearrange("p o n -> p (o n)")).then_inc(s_gb[b % 2], 16)

            for n, (kind, i, _) in enumerate(PIECES):
                if kind != "x":
                    load(kind, i)
                if n == 1:
                    for b in range(B):
                        sp.dma_start(ev[:, b, :], expert_vecs[bass.ds(role[b], 1), :, :]
                                     .rearrange("o p n -> p (o n)")).then_inc(s_ev, 16)
                    for b in range(B):
                        sp.dma_start(full[b:b + 1, :, :].rearrange("p a b -> p (a b)"),
                                     expert_rows[bass.ds(role[b], 1), 0:2 * V]).then_inc(s_rows, 16)
                        sp.dma_start(yn[b:b + 1, 0, 0, :],
                                     expert_rows[bass.ds(role[b], 1), 2 * V:3 * V]).then_inc(s_rows, 16)
                if n == 20:
                    gamma_beta(0)
                    gamma_beta(1)
            for kind, i in ORDER:
                if kind != "F":
                    continue
                b = i[1]
                for tt in range(TT):
                    sp.wait_ge(dve["F"], TT * (nth("F", i) - 1) + tt + 1)
                    sp.dma_start(out[b, tt * P:(tt + 1) * P, :], res[:, b, tt, :]).then_inc(s_out, 16)
                if b < 2:
                    gamma_beta(b + 2)
            sp.wait_ge(s_out, 16 * B * TT)

        @block.gpsimd
        def _(pool):
            link = [0]

            def step(ins):
                link[0] += 1
                ins.then_inc(pool_eps, 1)
                pool.wait_ge(pool_eps, link[0])

            eye = yn[:, 1, 0, 0:P]
            pool.memset(eye, 0.0).then_inc(pool_zero, 1)
            pool.memset(prob[:, :, :], 1.0).then_inc(pool_zero, 1)
            pool.memset(mhalf[:, :], -0.5).then_inc(pool_const, 1)
            pool.iota(feat_i[:, :], pattern=[[P, KF]], base=0, channel_multiplier=1).then_inc(pool_const, 1)
            pool.wait_ge(pool_zero, 2)
            pool.affine_select(out=eye, in_=eye, compare_op=ALU.not_equal, fill=1.0, base=0,
                               pattern=[[-1, P]], channel_multiplier=1).then_inc(pool_const, 1)
            for b in range(B):
                pool.affine_select(out=prob[:, b // 2, (b % 2) * P:(b % 2 + 1) * P],
                                   in_=prob[:, b // 2, (b % 2) * P:(b % 2 + 1) * P],
                                   compare_op=ALU.is_equal, fill=0.0, base=-b,
                                   pattern=[[0, P]], channel_multiplier=1).then_inc(pool_const, 1)
            for kind, i in ORDER:
                if kind == "W" and who_of[i] == "P":
                    slot = slot_of[i]
                    pool.wait_ge(s_raw[slot], 16 * use_of_slot[i])
                    for s, v in target_free(i):
                        pool.wait_ge(s, v)
                    pool.tensor_scalar(split_target(i, HI), raw[:, slot, :], 1.0, 0.0, ALU.mult, ALU.add)\
                        .then_inc(pool_hi, 1)
                    pool.wait_ge(pool_hi, split_count[i])
                    pool.tensor_tensor(split_target(i, LO), raw[:, slot, :], split_target(i, HI).bitcast(F32),
                                       ALU.subtract).then_inc(pool_w, 1)
                if kind == "U":
                    n = li[i[0]]
                    pool.wait_ge(dve["U"], nth("U", i))
                    pool.tensor_tensor(rstd[:, n, i[1], :], veps[:, n, i[1], :], mhalf[:, :], ALU.pow)\
                        .then_inc(pool_rstd, 1)

        @block.scalar
        def _(a):
            for b in range(B):
                slot = slot_of[("x", b)]
                if prev_in_slot[("x", b)]:
                    continue
                a.dma_start(raw[:, slot, :], xs[b, :, :]).then_inc(s_raw[slot], 16)
            a.dma_start(code_i[:, :], codes.partition_broadcast(P).rearrange("p o n -> p (o n)")).then_inc(s_code, 16)
            a.dma_start(sv[:, :], vecs).then_inc(s_vec, 16)
            late_x = [b for b in range(B) if prev_in_slot[("x", b)]]

            def gelu_pair(hi, whole, src, bias, done):
                a.activation(hi, src, ACT.Gelu, bias=bias).then_inc(done, 1)
                a.activation(whole, src, ACT.Gelu, bias=bias).then_inc(done, 1)

            for kind, i in ORDER:
                if kind == "W" and who_of[i] == "AV":
                    slot = slot_of[i]
                    a.wait_ge(s_raw[slot], 16 * use_of_slot[i])
                    for s, v in target_free(i):
                        a.wait_ge(s, v)
                    a.activation(split_target(i, HI), raw[:, slot, :], ACT.Copy).then_inc(act_w, 1)
                    for b in late_x:
                        if prev_in_slot[("x", b)] == i:
                            a.wait_ge(*split_done(i))
                            s2 = slot_of[("x", b)]
                            a.dma_start(raw[:, s2, :], xs[b, :, :]).then_inc(s_raw[s2], 16)
                elif kind == "D":
                    l, b = i
                    k = nth("D", i)
                    if k == 1:
                        a.wait_ge(s_ev, 16 * B)
                    a.wait_ge(pe["D"], k)
                    if k >= 2:
                        a.wait_ge(dve["D"], k - 1)
                    if k >= 3:
                        a.wait_ge(pe["U"], k - 2)
                    gelu_pair(act_h[:, k % 2, HI, :], act_full[:, :], bank("D", i, 2)[:, 0, :],
                              ev[:, b, BD[l]:BD[l] + 1], act["D"])
                elif kind == "N":
                    l, b = i
                    k = nth("N", i)
                    a.wait_ge(dve["N"], k)
                    if k >= 3:
                        a.wait_ge(pe["T"], k - 2)
                    for tt in range(TT):
                        a.activation(yn[:, k % 2, tt, :], bank("U", i)[:, tt, :], ACT.Identity,
                                     scale=rstd[:, li[l], b, tt:tt + 1], bias=nmr[:, li[l], b, tt:tt + 1])\
                            .then_inc(act["N"], 1)
                elif kind == "T":
                    l, b = i
                    k = nth("T", i)
                    a.wait_ge(pe["T"], k)
                    if l == 2 and k > B + 1:
                        a.wait_ge(dve["T"], 2 * (k - 1))
                    for kf in range(KF):
                        a.activation(layer_out(l, b)[:, kf, :], bank("T", i)[:, kf, :], ACT.Identity,
                                     scale=ev[:, b, GAMMA[l] + kf:GAMMA[l] + kf + 1],
                                     bias=ev[:, b, BETA[l] + kf:BETA[l] + kf + 1]).then_inc(act["T"], 1)
                elif kind in ("MN", "Y", "V", "PT"):
                    k = nth(kind, i)
                    a.wait_ge(pe[kind], k)
                    if kind == "Y" and k >= 2:
                        a.wait_ge(pe["S"], k - 1)
                    if kind == "PT" and k >= 2:
                        a.wait_ge(pe["A"], k - 1)
                    if kind == "V" and k >= 3:
                        a.wait_ge(pe["A"], k - 2)
                    a.activation(pair(kind, i, HI), bank(kind, i), ACT.Copy).then_inc(act[kind], 1)
                elif kind == "E":
                    k = nth("E", i)
                    a.wait_ge(dve["max"], k)
                    if k == 1:
                        a.wait_ge(dve_const, 1)
                    else:
                        a.wait_ge(pe["PT"], k - 1)
                    for tt in range(TT):
                        a.activation(prob[:, tt, :], bank("S", i)[:, tt, :], ACT.Exp, bias=nmax[:, i, tt:tt + 1],
                                     scale=V ** -0.5, accum_out=ssum[:, i, tt:tt + 1]).then_inc(act["E"], 1)
                elif kind == "A":
                    if nth("A", i) == 1:
                        a.wait_ge(s_vec, 16)
                    a.wait_ge(pe["A"], nth("A", i))
                    for kf in range(KF):
                        a.activation(attn_of(i, HI, kf), bank("A", i)[:, kf, :], ACT.Identity,
                                     bias=sv[:, BP + kf:BP + kf + 1]).then_inc(act["A"], 1)
                elif kind in ("H1", "H2B"):
                    phase = 0 if kind == "H1" else 1
                    m = hid(phase, *i)
                    a.wait_ge(pe["hidden"], m + 1)
                    if m >= HID_SLOTS:
                        a.wait_ge(pe["hidden_used"], m + 1 - HID_SLOTS)
                    if m >= 2:
                        a.wait_ge(dve["hidden"], m - 1)
                    src = ring[bank_of[("H1" if phase == 0 else "H2A", i)]][:, :]
                    bias = (MB1 if phase else CB1) + i[1]
                    gelu_pair(hidden[:, m % HID_SLOTS, HI, :], hidden_full[:, m % 2, :], src,
                              sv[:, bias:bias + 1], act["hidden"])
                elif kind == "CE":
                    a.wait_ge(pe["hidden_used"], hid(0, i, HT - 1) + 1)
                    if i >= 1:
                        a.wait_ge(pe["hidden"], hid(1, i - 1, HT - 1) + 1)
                    if i == 0:
                        a.wait_ge(dve_const, 2)
                    for kf in range(KF):
                        for j in range(CB):
                            a.activation(cms[:, HI, kf, j * S:(j + 1) * S], acc[:, kf, j * S:(j + 1) * S],
                                         ACT.Identity, bias=cbias[:, kf, CB * i + j:CB * i + j + 1])\
                                .then_inc(act["CE"], 1)

        @block.vector
        def _(v):
            link = [0]

            def step(ins):
                link[0] += 1
                ins.then_inc(dve_link, 1)
                v.wait_ge(dve_link, link[0])

            v.wait_ge(pool_const, 3 + B)
            v.tensor_copy(ident_r[:, :], yn[:, 1, 0, 0:P]).then_inc(dve_rows, 1)
            v.tensor_copy(ones_row[:, :, :].rearrange("p b n -> p (b n)"),
                          prob[:, :, :].rearrange("p a b -> p (a b)")).then_inc(dve_const, 1)

            def bias_rows():
                v.memset(rows[:, :, :, :].bitcast(F32), 0.0).then_inc(dve_link, 1)
                link[0] += 1
                v.wait_ge(dve_link, link[0])
                v.wait_ge(s_rows, 32 * B)
                v.tensor_copy(rows[0:B, HI, 0:2, :], full[0:B, :, :]).then_inc(dve_link, 1)
                v.tensor_copy(rows[0:B, HI, 2, :], yn[0:B, 0, 0, :]).then_inc(dve_link, 1)
                link[0] += 2
                v.wait_ge(dve_link, link[0])
                step(v.tensor_tensor(rows[0:B, LO, 0:2, :], full[0:B, :, :], rows[0:B, HI, 0:2, :].bitcast(F32),
                                     ALU.subtract))
                v.tensor_tensor(rows[0:B, LO, 2, :], yn[0:B, 0, 0, :], rows[0:B, HI, 2, :].bitcast(F32),
                                ALU.subtract).then_inc(dve_rows, 1)

            def cms_biases():
                v.wait_ge(s_code, 16)
                v.wait_ge(s_vec, 16)
                step(v.tensor_copy(code_f[:, :], code_i[:, :]))
                step(v.tensor_copy(feat_f[:, :], feat_i[:, :]))
                for kf in range(KF):
                    step(v.tensor_scalar(cbias[:, kf, :], code_f[:, :], feat_f[:, kf:kf + 1],
                                         sv[:, CB2 + kf:CB2 + kf + 1], ALU.is_equal, ALU.add))
                    ins = v.tensor_scalar(rbias[:, kf, :], cbias[:, kf, :], sv[:, MB2 + kf:MB2 + kf + 1], None, ALU.add)
                    if kf == 0:
                        step(ins)
                ins.then_inc(dve_const, 1)

            for kind, i in ORDER:
                if kind == "W" and who_of[i] == "AV":
                    v.wait_ge(act_w, split_count[i])
                    v.tensor_tensor(split_target(i, LO), raw[:, slot_of[i], :], split_target(i, HI).bitcast(F32),
                                    ALU.subtract).then_inc(dve_w, 1)
                elif kind == "D":
                    k = nth("D", i)
                    if k == 1:
                        bias_rows()
                    v.wait_ge(act["D"], 2 * k)
                    v.tensor_tensor(act_h[:, k % 2, LO, :], act_full[:, :], act_h[:, k % 2, HI, :].bitcast(F32),
                                    ALU.subtract).then_inc(dve["D"], 1)
                elif kind == "U":
                    l, b = i
                    n = li[l]
                    v.wait_ge(pe["U"], nth("U", i))
                    for tt in range(TT):
                        v.bn_stats(bn[:, b, tt, :], bank("U", i)[:, tt, :]).then_inc(dve_link, 1)
                        link[0] += 1
                    for tt in range(TT):
                        v.wait_ge(dve_link, link[0] - TT + 1 + 2 * tt if tt == 0 else link[0])
                        v.bn_aggr(mv[:, n, b, tt, :], bn[:, b, tt, :]).then_inc(dve_link, 1)
                        link[0] += 1
                    v.wait_ge(dve_link, link[0])
                    v.tensor_scalar(veps[:, n, b, :], mv[:, n, b, :, 1], LN_EPS, None, ALU.add)\
                        .then_inc(dve["U"], 1)
                elif kind == "N":
                    l, b = i
                    n = li[l]
                    v.wait_ge(pool_rstd, nth("U", i))
                    v.scalar_tensor_tensor(out=nmr[:, n, b, :], in0=mv[:, n, b, :, 0], scalar=-1.0,
                                           in1=rstd[:, n, b, :], op0=ALU.mult, op1=ALU.mult).then_inc(dve["N"], 1)
                elif kind == "T":
                    l, b = i
                    k = nth("T", i)
                    v.wait_ge(act["T"], KF * k)
                    if l == 0 and b >= 2:
                        v.wait_ge(pe["S"], nth("S", b - 2))
                        v.wait_ge(pe["V"], nth("V", b - 2))
                    if l == 2 and b < 2:
                        v.wait_ge(pe["S"], nth("S", b + 2))
                        v.wait_ge(pe["V"], nth("V", b + 2))
                    if l == 2 and b >= 2:
                        v.wait_ge(pe["U"], nth("U", (3, b - 2)))
                    v.tensor_copy(xmid[:, HI, b % 2], layer_out(l, b)[:, :, :]).then_inc(dve["T"], 1)
                    v.wait_ge(dve["T"], 2 * k - 1)
                    v.tensor_tensor(xmid[:, LO, b % 2], layer_out(l, b)[:, :, :], xmid[:, HI, b % 2].bitcast(F32),
                                    ALU.subtract).then_inc(dve["T"], 1)
                elif kind in ("MN", "Y", "V", "PT"):
                    v.wait_ge(act[kind], nth(kind, i))
                    v.tensor_tensor(pair(kind, i, LO), bank(kind, i), pair(kind, i, HI).bitcast(F32),
                                    ALU.subtract).then_inc(dve[kind], 1)
                elif kind == "S":
                    v.wait_ge(pe["S"], nth("S", i))
                    step(v.tensor_reduce(smax[:, i, :], bank("S", i), AX_X, ALU.max))
                    v.tensor_scalar(nmax[:, i, :], smax[:, i, :], -V ** -0.5, None, ALU.mult).then_inc(dve["max"], 1)
                elif kind == "E":
                    v.wait_ge(act["E"], TT * nth("E", i))
                    step(v.reciprocal(rsum[:, i, :], ssum[:, i, :]))
                    for tt in range(TT):
                        v.tensor_scalar(prob[:, tt, :], prob[:, tt, :], rsum[:, i, tt:tt + 1], None, ALU.mult)\
                            .then_inc(dve["E"], 1)
                    if i == B - 1:
                        cms_biases()
                elif kind == "A":
                    v.wait_ge(act["A"], KF * nth("A", i))
                    for kf in range(KF):
                        v.scalar_tensor_tensor(out=attn_of(i, LO, kf), in0=bank("A", i)[:, kf, :],
                                               scalar=sv[:, BP + kf:BP + kf + 1], in1=attn_of(i, HI, kf).bitcast(F32),
                                               op0=ALU.add, op1=ALU.subtract).then_inc(dve["A"], 1)
                elif kind in ("H1", "H2B"):
                    m = hid(0 if kind == "H1" else 1, *i)
                    v.wait_ge(act["hidden"], 2 * (m + 1))
                    v.tensor_tensor(hidden[:, m % HID_SLOTS, LO, :], hidden_full[:, m % 2, :],
                                    hidden[:, m % HID_SLOTS, HI, :].bitcast(F32), ALU.subtract)\
                        .then_inc(dve["hidden"], 1)
                elif kind == "CE":
                    n = 0
                    for kf in range(KF):
                        n += CB
                        v.wait_ge(act["CE"], CB * KF * i + n)
                        for j in range(CB):
                            b = CB * i + j
                            v.scalar_tensor_tensor(out=cms[:, LO, kf, j * S:(j + 1) * S],
                                                   in0=acc[:, kf, j * S:(j + 1) * S], scalar=cbias[:, kf, b:b + 1],
                                                   in1=cms[:, HI, kf, j * S:(j + 1) * S].bitcast(F32),
                                                   op0=ALU.add, op1=ALU.subtract).then_inc(dve["CE"], 1)
                    for j in range(CB):
                        for kf in range(KF):
                            b = CB * i + j
                            v.scalar_tensor_tensor(out=res[:, b, kf, :], in0=acc[:, kf, j * S:(j + 1) * S],
                                                   scalar=rbias[:, kf, b:b + 1], in1=res[:, b, kf, :],
                                                   op0=ALU.add, op1=ALU.add).then_inc(dve["CE"], 1)
                elif kind == "ME":
                    k = nth("ME", i)
                    j = i % CB
                    v.wait_ge(pe["hidden_used"], hid(1, i // CB, HT - 1) + 1)
                    v.wait_ge(dve["CE"], 2 * CB * KF * (i // CB + 1))
                    v.tensor_tensor(res[:, i], acc[:, :, j * S:(j + 1) * S], res[:, i], ALU.add)\
                        .then_inc(dve["z"], 1)
                    v.wait_ge(dve["z"], k)
                    if i < 2:
                        v.wait_ge(pe["U"], nth("U", (0, i + 2)))
                    else:
                        v.wait_ge(pe["U"], nth("U", (2, i - 2)))
                    v.tensor_scalar(xin[:, HI, i % 2], res[:, i], 0.0, 1.0, ALU.max, ALU.min)\
                        .then_inc(dve["ME"], 1)
                    v.tensor_scalar(res[:, i], res[:, i], 0.0, 1.0, ALU.max, ALU.min).then_inc(dve["ME"], 1)
                    v.wait_ge(dve["ME"], 3 * k - 1)
                    v.tensor_tensor(xin[:, LO, i % 2], res[:, i], xin[:, HI, i % 2].bitcast(F32), ALU.subtract)\
                        .then_inc(dve["ME"], 1)
                elif kind == "F":
                    l, b = i
                    n = li[l]
                    k = nth("F", i)
                    v.wait_ge(pool_rstd, nth("U", i))
                    v.wait_ge(s_gb[b % 2], 16 * (b // 2 + 1))
                    for tt in range(TT):
                        step(v.scalar_tensor_tensor(out=res[:, b, tt, :], in0=bank("U", i)[:, tt, :],
                                                    scalar=mv[:, n, b, tt, 0:1], in1=gb[:, b % 2, 0, :],
                                                    op0=ALU.subtract, op1=ALU.mult))
                        v.scalar_tensor_tensor(out=res[:, b, tt, :], in0=res[:, b, tt, :],
                                               scalar=rstd[:, n, b, tt:tt + 1], in1=gb[:, b % 2, 1, :],
                                               op0=ALU.mult, op1=ALU.add).then_inc(dve["F"], 1)

        @block.tensor
        def _(t):
            def take(step):
                if before[step]:
                    for s, n in freed(before[step]):
                        t.wait_ge(s, n)

            def products(out, pairs):
                todo = [(lhs(p), rhs(q)) for lhs, rhs in pairs for p, q in PASSES]
                for n, (l, r) in enumerate(todo):
                    ins = t.matmul(out, l, r, start=(n == 0), stop=(n == len(todo) - 1))
                return ins

            for kind, i in ORDER:
                if (kind, i) in bank_of:
                    take((kind, i))
                if kind == "D":
                    l, b = i
                    t.wait_ge(*split_done(("adp", i)))
                    if l == 0:
                        t.wait_ge(*split_done(("x", b)))
                    elif l == 2:
                        t.wait_ge(dve["ME"], 3 * nth("ME", b))
                    else:
                        t.wait_ge(dve["T"], 2 * nth("T", (2, b)))
                    products(bank("D", i)[:, 0, :],
                             [(lambda p, kf=kf: adp[:, p, adp_slot[i], kf * P:(kf + 1) * P],
                               lambda p, kf=kf: layer_in(l, b, p)[:, kf, :]) for kf in range(KF)])\
                        .then_inc(pe["D"], 1)
                elif kind == "U":
                    l, b = i
                    k = nth("D", i)
                    if nth("U", i) == 1:
                        t.wait_ge(dve_rows, 2)
                        t.wait_ge(dve_const, 1)
                    for tt in range(TT):
                        o = bank("U", i)[:, tt, :]
                        t.matmul(o, ones_row[:, b, :], rows[:, HI, li[l], :], start=True, stop=False)
                        t.matmul(o, ones_row[:, b, :], rows[:, LO, li[l], :], start=False, stop=False)
                        for p in (HI, LO):
                            for kf in range(KF):
                                t.matmul(o[:, kf * P:(kf + 1) * P], layer_in(l, b, p)[:, kf, tt * P:(tt + 1) * P],
                                         ident_r[:, :], start=False, stop=False)
                        if tt == 0:
                            t.wait_ge(dve["D"], k)
                        for n, (p, q) in enumerate(PASSES):
                            ins = t.matmul(o, act_h[:, k % 2, p, tt * P:(tt + 1) * P],
                                           adp[:, q, adp_slot[i], KF * P:KF * P + V],
                                           start=False, stop=(n == len(PASSES) - 1))
                    ins.then_inc(pe["U"], 1)
                elif kind == "T":
                    k = nth("N", i)
                    t.wait_ge(act["N"], TT * k)
                    for kf in range(KF):
                        for tt in range(TT):
                            ins = t.transpose(bank("T", i)[:, kf, tt * P:(tt + 1) * P],
                                              yn[:, k % 2, tt, kf * P:(kf + 1) * P], ident)
                    ins.then_inc(pe["T"], 1)
                elif kind == "MN":
                    for j in (2 * i, 2 * i + 1):
                        t.wait_ge(*split_done(("mn", j)))
                    for it in range(KF):
                        ins = products(bank("MN", i)[:, it, :],
                                       [(lambda p, kd=kd: w4[:, p, 4 * i + kd, it * P:(it + 1) * P],
                                         lambda p, kd=kd: w4[:, p, 4 * i + 2 + kd, :]) for kd in range(KF)])
                    ins.then_inc(pe["MN"], 1)
                elif kind == "Y":
                    b = i
                    t.wait_ge(dve["T"], 2 * nth("T", (0, b)))
                    t.wait_ge(dve["MN"], 1)
                    for jt in range(KF):
                        ins = products(bank("Y", i)[:, jt, :],
                                       [(lambda p, kf=kf: mn[:, p, 0, kf, jt * P:(jt + 1) * P],
                                         lambda p, kf=kf: xmid[:, p, b % 2, kf, :]) for kf in range(KF)])
                    ins.then_inc(pe["Y"], 1)
                elif kind == "V":
                    b = i
                    t.wait_ge(dve["MN"], 2)
                    for tt in range(TT):
                        ins = products(bank("V", i)[:, tt, :],
                                       [(lambda p, kf=kf: xmid[:, p, b % 2, kf, tt * P:(tt + 1) * P],
                                         lambda p, kf=kf: mn[:, p, 1, kf, :]) for kf in range(KF)])
                    ins.then_inc(pe["V"], 1)
                elif kind == "S":
                    b = i
                    t.wait_ge(dve["Y"], nth("Y", i))
                    for tt in range(TT):
                        ins = products(bank("S", i)[:, tt, :],
                                       [(lambda p, kf=kf: qk[:, p, kf, tt * P:(tt + 1) * P],
                                         lambda p, kf=kf: xmid[:, p, b % 2, kf, :]) for kf in range(KF)])
                    ins.then_inc(pe["S"], 1)
                elif kind == "PT":
                    t.wait_ge(dve["E"], TT * nth("E", i))
                    for ts in range(TT):
                        for tt in range(TT):
                            ins = t.transpose(bank("PT", i)[:, ts, tt * P:(tt + 1) * P],
                                              prob[:, tt, ts * P:(ts + 1) * P], ident)
                    ins.then_inc(pe["PT"], 1)
                elif kind == "A":
                    b = i
                    t.wait_ge(dve["PT"], nth("PT", i))
                    t.wait_ge(dve["V"], nth("V", i))
                    for jt in range(KF):
                        ins = products(bank("A", i)[:, jt, :],
                                       [(lambda p, ts=ts: vv[:, p, b % 2, ts, jt * P:(jt + 1) * P],
                                         lambda p, ts=ts: probT[:, p, ts, :]) for ts in range(TT)])
                    ins.then_inc(pe["A"], 1)
                elif kind == "H1":
                    c, ht = i
                    t.wait_ge(*split_done(("w", ht // 2)))
                    if ht == 0:
                        t.wait_ge(dve["A"], KF * nth("A", CB * c + CB - 1))
                    products(ring[bank_of[(kind, i)]][:, :],
                             [(lambda p, kf=kf: w1[:, p, ht, kf, :],
                               lambda p, kf=kf: attn[:, c, p, kf, :]) for kf in range(KF)])\
                        .then_inc(pe["hidden"], 1)
                elif kind == "H2A":
                    c, ht = i
                    t.wait_ge(*split_done(("w", 8 + ht)))
                    o = ring[bank_of[(kind, i)]][:, :]
                    n = 0
                    for kf in range(KF):
                        for p, q in PASSES:
                            t.matmul(o, w3[:, p, ht, kf, :], attn[:, c, q, kf, :], start=(n == 0), stop=False)
                            n += 1
                elif kind == "H2B":
                    c, ht = i
                    if ht == 0:
                        t.wait_ge(dve["CE"], 2 * CB * KF * c + CB * KF)
                    o = ring[bank_of[("H2A", i)]][:, :]
                    n = 0
                    for kf in range(KF):
                        for p, q in PASSES:
                            ins = t.matmul(o, w3[:, p, ht, KF + kf, :], cms[:, q, kf, :], start=False,
                                           stop=(n == KF * len(PASSES) - 1))
                            n += 1
                    ins.then_inc(pe["hidden"], 1)
                elif kind in ("CMS", "MOD"):
                    c, ht = i
                    phase = 0 if kind == "CMS" else 1
                    w, m = (w4 if phase else w2), hid(phase, c, ht)
                    t.wait_ge(*split_done(("w", (16 if phase else 4) + ht // 2)))
                    t.wait_ge(dve["hidden"], m + 1)
                    if ht == 0 and phase == 1:
                        t.wait_ge(dve["CE"], 2 * CB * KF * (c + 1))
                    if ht == 0 and phase == 0 and c >= 1:
                        t.wait_ge(dve["z"], nth("ME", CB * c - 1))
                    for ft in range(KF):
                        for n, (p, q) in enumerate(PASSES):
                            ins = t.matmul(acc[:, ft, :], w[:, p, ht, ft * P:(ft + 1) * P],
                                           hidden[:, m % HID_SLOTS, q, :], start=(ht == 0 and n == 0),
                                           stop=(ht == HT - 1 and n == len(PASSES) - 1))
                    ins.then_inc(pe["hidden_used"], 1)



def kernel(**inputs):
    import numpy as np
    import concourse.bacc as bacc
    from concourse.bass_utils import run_bass_kernel_spmd as run

    a = {k: np.asarray(v) for k, v in inputs.items()}
    out_shape = a["x"].shape

    def tiles(w):
        return w.reshape(w.shape[0] // P, P, w.shape[1]).transpose(1, 0, 2)

    def columns(*vecs):
        return np.concatenate([u.reshape(-1, P).T for u in vecs], axis=1)

    def cut(w):
        return w.reshape(P, -1, PIECE).transpose(1, 0, 2)

    def hidden_tiles(w):
        k, h = w.shape
        return w.reshape(k // P, P, h // P, P).transpose(1, 2, 0, 3).reshape(P, -1)

    weights = np.concatenate([
        np.stack([tiles(a["L1_cond_" + n].T if n != "Wp" else a["L1_cond_Wp"]).reshape(P, PIECE)
                  for n in ("Wq", "Wk", "Wv", "Wp")]),
        cut(hidden_tiles(a["L1_cond_cW1"])), cut(tiles(a["L1_cond_cW2"]).reshape(P, -1)),
        cut(hidden_tiles(a["L1_cond_mW1"])), cut(tiles(a["L1_cond_mW2"]).reshape(P, -1))])
    adapters = np.stack([
        np.concatenate([tiles(a[f"L{l}_cond_W_down"][e]).reshape(P, -1), a[f"L{l}_cond_W_up"][e]], axis=1)
        for l in LAYERS for e in range(E)])
    expert_vecs = np.stack([columns(
        a["L0_cond_b_down"][e], a["L0_cond_gamma"][e], a["L0_cond_beta"][e],
        a["L2_cond_b_down"][e], a["L2_cond_ln_w"][e], a["L2_cond_ln_b"][e],
        a["L3_cond_b_down"][e]) for e in range(E)])
    expert_rows = np.concatenate([a["L0_cond_b_up"], a["L2_cond_b_up"], a["L3_cond_b_up"],
                                  a["L3_cond_gamma"], a["L3_cond_beta"]], axis=1)
    vecs = columns(*(a["L1_cond_" + n] for n in ("cb1", "mb1", "bp", "cb2", "mb2")))
    xs = a["x"].transpose(0, 2, 1).reshape(B, KF, P, S).transpose(0, 2, 1, 3).reshape(B, P, KF * S)
    arrays = {
        "roles": a["itok_B_1_2"].reshape(1, B), "codes": a["itok_B_17_1546"].reshape(1, B),
        "xs": xs, "weights": weights, "adapters": adapters, "expert_vecs": expert_vecs,
        "expert_rows": expert_rows, "vecs": vecs}
    arrays = {f"in_{k}": np.ascontiguousarray(v) for k, v in arrays.items()}

    nc = bacc.Bacc("TRN2", target_bir_lowering=False, num_devices=1, dynamic_dma_scratch_size=1024)
    args = [nc.dram_tensor(k, v.shape, mybir.dt.from_np(v.dtype), kind="ExternalInput").ap()
            for k, v in arrays.items()]
    out = nc.dram_tensor("out_x", out_shape, F32, kind="ExternalOutput").ap()
    build(nc, *args, out)
    r = run(nc, [arrays], core_ids=[0])
    return r.results[0]["out_x"]
```

```python
from contextlib import ExitStack

import concourse.bass as bass
from concourse import mybir

P = 128
F32 = mybir.dt.float32
F32R = mybir.dt.float32r
I32 = mybir.dt.int32
ALU = mybir.AluOpType
ACT = mybir.ActivationFunctionType
AX_X = mybir.AxisListType.X

B, S, V = 4, 256, 256
KF = V // P
TT = S // P
CB = 2
NC = B // CB
CT = CB * S
HT = 4 * V // P
E = 3
LN_EPS = 1e-5
HI, LO = 0, 1
LO_ROW = 32
PASSES = ((HI, HI), (HI, LO), (LO, HI))
PIECE = 512
RAW_SLOTS = 6
ADP_SLOTS = 4
HID_SLOTS = 3
RING = 6
LAYERS = (0, 2, 3)

BD = {0: 0, 2: 5, 3: 10}
GAMMA = {0: 1, 2: 6}
BETA = {0: 3, 2: 8}
EV = 11
CB1, MB1, BP, CB2, MB2 = 0, HT, 2 * HT, 2 * HT + KF, 2 * HT + 2 * KF
SV = 2 * HT + 3 * KF


def splitter(piece):
    kind, i = piece
    if kind == "x" or (kind == "adp" and i[0] == 0) or (kind == "mn" and i >= 2):
        return "AV"
    return "P"


def diagonals(chain, n):
    for d in range(len(chain) + n - 1):
        yield [(kind, d - k) for k in reversed(range(len(chain))) if 0 <= d - k < n for kind in chain[k]]


def order():
    o = []

    def split(kind, i):
        o.append(("W", (kind, i)))

    weights = iter(range(20))
    for d, steps in enumerate(diagonals([("D",), ("U",), ("N",), ("T",), ("Y",), ("S", "E", "V"), ("PT",), ("A",)], B)):
        for b in ((0, 1) if d == 0 else (d + 1,) if d + 1 < B else ()):
            split("x", b)
            split("adp", (0, b))
            o.append(("ROWS", b))
        if d < 2:
            split("mn", 2 * d)
            split("mn", 2 * d + 1)
        for kind, b in steps:
            o.append((kind, (0, b) if kind in "DUNT" else b))
        if d in (2, 3):
            o.append(("MN", d - 2))
        for _ in range(1 if d < 4 else 2):
            split("w", next(weights))
    o.append(("CB", 0))
    later = [("W", ("w", n)) for n in weights] + [("W", ("adp", (l, b))) for b in range(CB) for l in (2, 3)]
    last = [("W", ("adp", (l, b))) for b in range(CB, B) for l in (2, 3)]

    def adapters(bs):
        chain = [[("D", 2)], [("U", 2)], [("N", 2)], [("T", 2)], [("D", 3)], [("U", 3)], [("F", 3)]]
        return [(kind, (l, bs[j])) for steps in diagonals(chain, len(bs)) for (kind, l), j in steps]

    mlp = []
    for c in range(NC):
        ends = [("MOD", (c - 1, HT - 2)), ("MOD", (c - 1, HT - 1))] if c else []
        for ht in range(HT):
            use = [("CMS", (c, ht - 2))] if ht >= 2 else ends[ht:ht + 1]
            mlp.append([("H1", (c, ht))] + use)
            if c and ht == 1:
                mlp[-1] += [("ME", b) for b in range(CB * (c - 1), CB * c)]
        mlp.append([("H2A", (c, 0)), ("CMS", (c, HT - 2))])
        mlp.append([("H2A", (c, 1)), ("CMS", (c, HT - 1)), ("CE", c)])
        mlp.append([("H2A", (c, 2)), ("H2A", (c, 3))])
        for ht in range(HT):
            mlp.append([("H2B", (c, ht))])
            if ht >= 2:
                mlp[-1].append(("MOD", (c, ht - 2)))
            if 1 <= ht and ht + 3 < HT:
                mlp[-1].append(("H2A", (c, ht + 3)))
    mlp.append([("MOD", (NC - 1, HT - 2))])
    mlp.append([("MOD", (NC - 1, HT - 1))] + [("ME", b) for b in range(CB * (NC - 1), B)])
    work = adapters(range(CB))
    first = len(mlp) // 2 + 1
    for n, group in enumerate(mlp):
        o.extend(group)
        if n > first and work:
            left = len(mlp) - n
            k = -(-len(work) // left)
            o.extend(work[:k])
            del work[:k]
        for _ in range(2):
            if later:
                o.append(later.pop(0))
        if n > first + 6 and last:
            o.append(last.pop(0))
    o.extend(later + work + last)
    o.extend(adapters(range(CB, B)))
    assert len(set(o)) == len(o)
    return o


def build(nc, roles, codes, xs, weights, adapters0, adapters, expert_rows, vecs, out):
    ORDER = order()
    PIECES = [(*i, splitter(i)) for kind, i in ORDER if kind == "W"]
    nth_of, seen = {}, {}
    for kind, i in ORDER:
        seen[kind] = seen.get(kind, 0) + 1
        nth_of[(kind, i)] = seen[kind]

    def nth(kind, i):
        return nth_of[(kind, i)]

    needed_until = {"U": ("N", "F"), "S": ("E",), "H2A": ("H2B",)}
    where = {step: n for n, step in enumerate(ORDER)}
    bank_of, before = {}, {}
    last, free_at = [None] * RING, [n - RING for n in range(RING)]
    for n, (kind, i) in enumerate(ORDER):
        if kind in ("D", "U", "T", "MN", "Y", "V", "S", "PT", "A", "H1", "H2A"):
            k = min(range(RING), key=lambda m: free_at[m])
            bank_of[(kind, i)], before[(kind, i)] = k, last[k]
            last[k] = (kind, i)
            free_at[k] = next(where[(q, i)] for q in needed_until.get(kind, (kind,)) if (q, i) in where)
            assert free_at[k] >= n

    def hid(phase, c, ht):
        return (c * 2 + phase) * HT + ht

    place_of, place_before, landing = {}, {}, {}
    users, n = {}, 0
    for kind, i, who in PIECES:
        if kind == "x":
            place = ("res", i)
        elif kind == "mn" and i >= 2:
            place = ("gb", i - 2)
        else:
            place = ("raw", n % RAW_SLOTS)
            n += 1
        place_of[(kind, i)] = place
        before_it = users.setdefault(place, [])
        place_before[(kind, i)] = before_it[-1] if before_it else None
        before_it.append((kind, i))
        landing[(kind, i)] = 16 * len(before_it)
    counts = {"AV": 0, "P": 0}
    split_count = {}
    who_of = {(k, i): w for k, i, w in PIECES}
    for kind, i in ORDER:
        if kind == "W":
            counts[who_of[i]] += 1
            split_count[i] = counts[who_of[i]]
    adp_pieces = [i for k, i, _ in PIECES if k == "adp"]
    adp_slot = {i: n % ADP_SLOTS for n, i in enumerate(adp_pieces)}
    adp_before = {i: (adp_pieces[n - ADP_SLOTS] if n >= ADP_SLOTS else None) for n, i in enumerate(adp_pieces)}

    with ExitStack() as ctx:
        def sb(name, shape, dt=F32):
            return ctx.enter_context(nc.sbuf_tensor(name, shape, dt))

        def sem(name):
            return ctx.enter_context(nc.semaphore(name))

        raw = sb("raw", [P, RAW_SLOTS, PIECE + EV])
        w1 = sb("w1", [P, 2, HT, KF, P], F32R)
        w2 = sb("w2", [P, 2, HT, V], F32R)
        w3 = sb("w3", [P, 2, HT, 2 * KF, P], F32R)
        w4 = sb("w4", [P, 2, HT, V], F32R)
        adp = sb("adp", [P, 2, ADP_SLOTS, PIECE], F32R)
        mn = sb("mn", [P, 2, 2, KF, V], F32R)
        xin = sb("xin", [P, 2, 2, KF, S], F32R)
        xmid = sb("xmid", [P, 2, 2, KF, S], F32R)
        res = sb("res", [P, B, KF, S])
        qk = sb("qk", [P, 2, KF, S], F32R)
        vv = sb("vv", [P, 2, 2, TT, V], F32R)
        prob = sb("prob", [P, TT, S])
        probT = sb("probT", [P, 2, TT, S], F32R)
        attn = sb("attn", [P, NC, 2, KF, CT], F32R)
        hidden = sb("hidden", [P, HID_SLOTS, 2, CT], F32R)
        hidden_full = sb("hidden_full", [P, 2, CT])
        cms = sb("cms", [P, 2, KF, CT], F32R)
        act_h = sb("act_h", [P, 2, 2, S], F32R)
        act_full = sb("act_full", [P, S])
        yn = sb("yn", [P, 2, TT, V])
        full = sb("full", [P, KF, S])
        gb = sb("gb", [P, 2, 2, V])
        rows = sb("rows", [P, B, V], F32R)
        ones_row = sb("ones_row", [P, 3, P], F32R)
        ident_r = sb("ident_r", [P, P], F32R)
        ident = ident_r[:, :].bitcast(F32)
        ev = sb("ev", [P, B, EV])
        sv = sb("sv", [P, SV])
        code_i = sb("code_i", [P, B], I32)
        code_f = sb("code_f", [P, B])
        feat_i = sb("feat_i", [P, KF], I32)
        feat_f = sb("feat_f", [P, KF])
        cbias = sb("cbias", [P, KF, B])
        rbias = sb("rbias", [P, KF, B])
        bn = sb("bn", [P, B, TT, 6])
        mv = sb("mv", [P, 3, B, TT, 2])
        veps = sb("veps", [P, 3, B, TT])
        rstd = sb("rstd", [P, 3, B, TT])
        nmr = sb("nmr", [P, 3, B, TT])
        mhalf = sb("mhalf", [P, TT])
        smax = sb("smax", [P, B, TT])
        nmax = sb("nmax", [P, B, TT])
        ssum = sb("ssum", [P, B, TT])
        rsum = sb("rsum", [P, B, TT])

        ring = [ctx.enter_context(nc.psum_tensor(f"ring{i}", [P, 512], F32)) for i in range(RING)]
        acc = ctx.enter_context(nc.psum_tensor("acc", [P, KF, CT], F32))

        def bank(kind, i, two=2):
            return ring[bank_of[(kind, i)]][:, :].rearrange("p (a b) -> p a b", a=two)

        s_raw = [sem(f"raw_landed{i}") for i in range(RAW_SLOTS)]
        s_vec, s_code = sem("vecs_landed"), sem("codes_landed")
        s_rows = [sem(f"rows_landed{b}") for b in range(B)]
        s_x = [sem(f"x_landed{b}") for b in range(B)]
        s_gb = [sem(f"gamma_beta_landed{i}") for i in range(2)]
        s_out = sem("out_landed")
        act_w, dve_w, pool_hi, pool_w = sem("act_W_hi"), sem("dve_W_lo"), sem("pool_W_hi"), sem("pool_W_lo")
        pool_zero, pool_const = sem("pool_zeros"), sem("pool_constants")
        dve_const, dve_rows, dve_link = sem("dve_constants"), sem("dve_rows"), sem("dve_link")
        pe = {k: sem(f"pe_{k}") for k in ("D", "U", "T", "MN", "Y", "V", "S", "PT", "A", "hidden", "hidden_used")}
        act = {k: sem(f"act_{k}") for k in ("D", "N", "T", "MN", "Y", "V", "E", "PT", "A", "hidden", "CE")}
        dve = {k: sem(f"dve_{k}") for k in
               ("D", "U", "N", "T", "MN", "Y", "V", "max", "E", "PT", "A", "hidden", "CE", "z", "ME", "F")}
        pool_rstd, act_first = sem("pool_rstd"), sem("act_first_gelu")
        pool_eps = sem("pool_link")

        def freed(step):
            kind, i = step
            k = nth(kind, i)
            if kind == "D":
                return [(act["D"], 2 * k)]
            if kind == "U":
                if i[0] == 3:
                    return [(dve["F"], 2 * nth("F", i))]
                return [(act["N"], TT * nth("N", i))]
            if kind == "T":
                return [(act["T"], KF * k)]
            if kind == "S":
                return [(act["E"], TT * k)]
            if kind in ("MN", "Y", "V", "PT"):
                return [(dve[kind], k)]
            if kind == "A":
                return [(dve["A"], KF * k)]
            m = hid(0 if kind == "H1" else 1, *i)
            return [(act["hidden"], 2 * (m + 1))]

        def split_done(piece):
            return (dve_w if who_of[piece] == "AV" else pool_w), split_count[piece]

        def source(piece):
            where, n = place_of[piece]
            if where == "res":
                return res[:, n]
            if where == "gb":
                return gb[:, n].rearrange("p a b -> p (a b)")
            return raw[:, n, 0:PIECE]

        def landed(piece):
            where, n = place_of[piece]
            return {"res": s_x, "gb": s_gb, "raw": s_raw}[where][n], landing[piece]

        def split_target(piece, part):
            kind, i = piece
            if kind == "x":
                return layer_in(0, i, part)
            if kind == "adp":
                return adp[:, part, adp_slot[i], :]
            if kind == "mn":
                return w4[:, part, 2 * i:2 * i + 2, :].rearrange("p a b -> p (a b)")
            if i < 4:
                return w1[:, part, 2 * i:2 * i + 2, :, :].rearrange("p a b c -> p (a b c)")
            if i < 8:
                return w2[:, part, 2 * (i - 4):2 * (i - 4) + 2, :].rearrange("p a b -> p (a b)")
            if i < 16:
                return w3[:, part, i - 8, :, :].rearrange("p a b -> p (a b)")
            return w4[:, part, 2 * (i - 16):2 * (i - 16) + 2, :].rearrange("p a b -> p (a b)")

        def target_free(piece):
            kind, i = piece
            if kind == "adp" and adp_before[i]:
                return [(pe["U"], nth("U", adp_before[i]))]
            if kind == "w" and i >= 16:
                return [(pe["MN"], 2)]
            return []

        def layer_in(l, b, part):
            if l == 0 and b >= CB:
                return attn[:, 1, part, :, (b - CB) * S:(b - CB + 1) * S]
            return (xmid if l == 3 else xin)[:, part, b % 2]

        def attn_of(b, part, kf):
            return attn[:, b // CB, part, kf, (b % CB) * S:(b % CB + 1) * S]

        def pair(kind, i, part):
            return {"MN": mn[:, part, i % 2], "Y": qk[:, part], "V": vv[:, part, i % 2],
                    "PT": probT[:, part]}[kind]

        def layer_out(l, b):
            return res[:, b] if l == 0 else full

        def landed_rows(b):
            return hidden_full[0:3, b // 2, (b % 2) * V:(b % 2 + 1) * V]

        li = {l: n for n, l in enumerate(LAYERS)}
        block = ctx.enter_context(nc.Block())

        @block.sync
        def _(sp):
            role = {}

            def load(kind, i):
                piece = (kind, i)
                if place_before[piece]:
                    sp.wait_ge(*split_done(place_before[piece]))
                if kind == "adp":
                    l, b = i
                    if b not in role:
                        role[b] = sp.value_load(roles[0:1, b:b + 1], min_val=0, max_val=E - 1)
                    if l == 0:
                        dst = raw[:, place_of[piece][1], :]
                        src = adapters0[bass.ds(role[b], 1), :, :].rearrange("o p n -> p (o n)")
                    else:
                        dst = source(piece)
                        src = adapters[bass.ds(role[b] + E * (li[l] - 1), 1), :, :].rearrange("o p n -> p (o n)")
                else:
                    dst = source(piece)
                    src = weights[{"mn": 0, "w": 4}[kind] + i, :, :]
                s, _ = landed(piece)
                sp.dma_start(dst, src).then_inc(s, 16)

            def gamma_beta(b):
                if b >= 2:
                    sp.wait_ge(dve["F"], 2 * nth("F", (3, b - 2)))
                else:
                    sp.wait_ge(*split_done(("mn", 2 + b)))
                sp.dma_start(gb[:, b % 2, :, :].rearrange("p a v -> p (a v)"),
                             expert_rows[bass.ds(role[b], 1), 3 * V:5 * V].partition_broadcast(P)
                             .rearrange("p o n -> p (o n)")).then_inc(s_gb[b % 2], 16)

            def load_rows(b):
                sp.dma_start(landed_rows(b), expert_rows[bass.ds(role[b], 1), 0:3 * V]
                             .rearrange("o (l n) -> (o l) n", l=3)).then_inc(s_rows[b], 16)

            first = [("adp", (0, 0)), ("adp", (0, 1))]
            rest = [(kind, i) for kind, i, _ in PIECES if (kind, i) not in first + [("x", 0), ("x", 1)]]
            for piece in first + rest:
                if piece[0] == "x":
                    sp.dma_start(source(piece), xs[piece[1], :, :].rearrange("p (a b) -> p a b", a=KF))\
                        .then_inc(landed(piece)[0], 16)
                else:
                    load(*piece)
                if piece[0] == "adp" and piece[1][0] == 0:
                    load_rows(piece[1][1])
                if piece == ("mn", 3):
                    sp.dma_start(sv[:, :], vecs).then_inc(s_vec, 16)
                    sp.dma_start(code_i[:, :], codes.partition_broadcast(P).rearrange("p o n -> p (o n)"))\
                        .then_inc(s_code, 16)
                if piece == ("w", 16):
                    gamma_beta(0)
                    gamma_beta(1)
            for kind, i in ORDER:
                if kind != "F":
                    continue
                b = i[1]
                for tt in range(TT):
                    sp.wait_ge(dve["F"], TT * (nth("F", i) - 1) + tt + 1)
                    sp.dma_start(out[b, tt * P:(tt + 1) * P, :], res[:, b, tt, :]).then_inc(s_out, 16)
                if b < 2:
                    gamma_beta(b + 2)
            sp.wait_ge(s_out, 16 * B * TT)

        @block.gpsimd
        def _(pool):
            link = [0]

            def step(ins):
                link[0] += 1
                ins.then_inc(pool_eps, 1)
                pool.wait_ge(pool_eps, link[0])

            eye = yn[:, 1, 0, 0:P]
            pool.memset(eye, 0.0).then_inc(pool_zero, 1)
            pool.wait_ge(pool_zero, 1)
            pool.affine_select(out=eye, in_=eye, compare_op=ALU.not_equal, fill=1.0, base=0,
                               pattern=[[-1, P]], channel_multiplier=1).then_inc(pool_const, 1)
            pool.memset(mhalf[:, :], -0.5).then_inc(pool_const, 1)
            pool.iota(feat_i[:, :], pattern=[[P, KF]], base=0, channel_multiplier=1).then_inc(pool_const, 1)
            for kind, i in ORDER:
                if kind == "W" and who_of[i] == "P":
                    pool.wait_ge(*landed(i))
                    for s, v in target_free(i):
                        pool.wait_ge(s, v)
                    pool.tensor_scalar(split_target(i, HI), source(i), 1.0, 0.0, ALU.mult, ALU.add)\
                        .then_inc(pool_hi, 1)
                    pool.wait_ge(pool_hi, split_count[i])
                    pool.tensor_tensor(split_target(i, LO), source(i), split_target(i, HI).bitcast(F32),
                                       ALU.subtract).then_inc(pool_w, 1)
                if kind == "U":
                    n = li[i[0]]
                    pool.wait_ge(dve["U"], nth("U", i))
                    pool.tensor_tensor(rstd[:, n, i[1], :], veps[:, n, i[1], :], mhalf[:, :], ALU.pow)\
                        .then_inc(pool_rstd, 1)

        @block.scalar
        def _(a):
            def load_x(b):
                a.dma_start(res[:, b].rearrange("p a b -> p (a b)"), xs[b, :, :]).then_inc(s_x[b], 16)

            load_x(0)
            load_x(1)

            a.wait_ge(dve_const, 1)
            a.activation(ssum[:, 0, :], nmax[:, 0, :], ACT.Gelu).then_inc(act_first, 1)

            def gelu_pair(hi, whole, src, bias, done):
                a.activation(hi, src, ACT.Gelu, bias=bias).then_inc(done, 1)
                a.activation(whole, src, ACT.Gelu, bias=bias).then_inc(done, 1)

            for kind, i in ORDER:
                if kind == "W" and who_of[i] == "AV":
                    a.wait_ge(*landed(i))
                    for s, v in target_free(i):
                        a.wait_ge(s, v)
                    a.activation(split_target(i, HI), source(i), ACT.Copy).then_inc(act_w, 1)
                elif kind == "D":
                    l, b = i
                    k = nth("D", i)
                    a.wait_ge(pe["D"], k)
                    if k >= 2:
                        a.wait_ge(dve["D"], k - 1)
                    if k >= 3:
                        a.wait_ge(pe["U"], k - 2)
                    gelu_pair(act_h[:, k % 2, HI, :], act_full[:, :], bank("D", i, 2)[:, 0, :],
                              ev[:, b, BD[l]:BD[l] + 1], act["D"])
                elif kind == "N":
                    l, b = i
                    k = nth("N", i)
                    a.wait_ge(dve["N"], k)
                    if k >= 3:
                        a.wait_ge(pe["T"], k - 2)
                    for tt in range(TT):
                        a.activation(yn[:, k % 2, tt, :], bank("U", i)[:, tt, :], ACT.Identity,
                                     scale=rstd[:, li[l], b, tt:tt + 1], bias=nmr[:, li[l], b, tt:tt + 1])\
                            .then_inc(act["N"], 1)
                elif kind == "T":
                    l, b = i
                    k = nth("T", i)
                    a.wait_ge(pe["T"], k)
                    if l == 2 and k > B + 1:
                        a.wait_ge(dve["T"], 2 * (k - 1))
                    for kf in range(KF):
                        a.activation(layer_out(l, b)[:, kf, :], bank("T", i)[:, kf, :], ACT.Identity,
                                     scale=ev[:, b, GAMMA[l] + kf:GAMMA[l] + kf + 1],
                                     bias=ev[:, b, BETA[l] + kf:BETA[l] + kf + 1]).then_inc(act["T"], 1)
                elif kind in ("MN", "Y", "V", "PT"):
                    k = nth(kind, i)
                    a.wait_ge(pe[kind], k)
                    if kind == "Y" and k >= 2:
                        a.wait_ge(pe["S"], k - 1)
                    if kind == "PT" and k >= 2:
                        a.wait_ge(pe["A"], k - 1)
                    if kind == "V" and k >= 3:
                        a.wait_ge(pe["A"], k - 2)
                    a.activation(pair(kind, i, HI), bank(kind, i), ACT.Copy).then_inc(act[kind], 1)
                elif kind == "E":
                    k = nth("E", i)
                    a.wait_ge(dve["max"], k)
                    if k >= 2:
                        a.wait_ge(pe["PT"], k - 1)
                    for tt in range(TT):
                        a.activation(prob[:, tt, :], bank("S", i)[:, tt, :], ACT.Exp, bias=nmax[:, i, tt:tt + 1],
                                     scale=V ** -0.5, accum_out=ssum[:, i, tt:tt + 1]).then_inc(act["E"], 1)
                elif kind == "A":
                    if nth("A", i) == 1:
                        a.wait_ge(s_vec, 16)
                    a.wait_ge(pe["A"], nth("A", i))
                    for kf in range(KF):
                        a.activation(attn_of(i, HI, kf), bank("A", i)[:, kf, :], ACT.Identity,
                                     bias=sv[:, BP + kf:BP + kf + 1]).then_inc(act["A"], 1)
                elif kind in ("H1", "H2B"):
                    phase = 0 if kind == "H1" else 1
                    m = hid(phase, *i)
                    a.wait_ge(pe["hidden"], m + 1)
                    if m >= HID_SLOTS:
                        a.wait_ge(pe["hidden_used"], m + 1 - HID_SLOTS)
                    if m >= 2:
                        a.wait_ge(dve["hidden"], m - 1)
                    src = ring[bank_of[("H1" if phase == 0 else "H2A", i)]][:, :]
                    bias = (MB1 if phase else CB1) + i[1]
                    gelu_pair(hidden[:, m % HID_SLOTS, HI, :], hidden_full[:, m % 2, :], src,
                              sv[:, bias:bias + 1], act["hidden"])
                elif kind == "CE":
                    a.wait_ge(pe["hidden_used"], hid(0, i, HT - 1) + 1)
                    if i >= 1:
                        a.wait_ge(pe["hidden"], hid(1, i - 1, HT - 1) + 1)
                    if i == 0:
                        a.wait_ge(dve_const, 6)
                    for kf in range(KF):
                        for j in range(CB):
                            a.activation(cms[:, HI, kf, j * S:(j + 1) * S], acc[:, kf, j * S:(j + 1) * S],
                                         ACT.Identity, bias=cbias[:, kf, CB * i + j:CB * i + j + 1])\
                                .then_inc(act["CE"], 1)

        @block.vector
        def _(v):
            link = [0]

            def step(ins):
                link[0] += 1
                ins.then_inc(dve_link, 1)
                v.wait_ge(dve_link, link[0])

            step(v.memset(rows[:, :, :].bitcast(F32), 0.0))
            v.memset(nmax[:, 0, :], 0.0).then_inc(dve_const, 1)
            def selectors():
                v.wait_ge(pool_const, 3)
                v.tensor_copy(ident_r[:, :], yn[:, 1, 0, 0:P]).then_inc(dve_const, 1)
                for l in range(3):
                    v.tensor_scalar(ones_row[:, l, :], rows[:, B - 1, 0:P].bitcast(F32), yn[:, 1, 0, l:l + 1],
                                    yn[:, 1, 0, LO_ROW + l:LO_ROW + l + 1], ALU.add, ALU.add).then_inc(dve_const, 1)

            def bias_rows(b):
                v.wait_ge(s_rows[b], 16)
                step(v.tensor_copy(rows[0:3, b, :], landed_rows(b)))
                v.tensor_tensor(rows[LO_ROW:LO_ROW + 3, b, :], landed_rows(b), rows[0:3, b, :].bitcast(F32),
                                ALU.subtract).then_inc(dve_rows, 1)

            def cms_biases():
                v.wait_ge(s_code, 16)
                v.wait_ge(s_vec, 16)
                step(v.tensor_copy(code_f[:, :], code_i[:, :]))
                step(v.tensor_copy(feat_f[:, :], feat_i[:, :]))
                for kf in range(KF):
                    step(v.tensor_scalar(cbias[:, kf, :], code_f[:, :], feat_f[:, kf:kf + 1],
                                         sv[:, CB2 + kf:CB2 + kf + 1], ALU.is_equal, ALU.add))
                    ins = v.tensor_scalar(rbias[:, kf, :], cbias[:, kf, :], sv[:, MB2 + kf:MB2 + kf + 1], None, ALU.add)
                    if kf == 0:
                        step(ins)
                ins.then_inc(dve_const, 1)

            for kind, i in ORDER:
                if kind == "W" and who_of[i] == "AV":
                    v.wait_ge(act_w, split_count[i])
                    if i[0] == "adp":
                        step(v.tensor_copy(ev[:, i[1][1], :], raw[:, place_of[i][1], PIECE:PIECE + EV]))
                    v.tensor_tensor(split_target(i, LO), source(i), split_target(i, HI).bitcast(F32),
                                    ALU.subtract).then_inc(dve_w, 1)
                elif kind == "D":
                    k = nth("D", i)
                    v.wait_ge(act["D"], 2 * k)
                    v.tensor_tensor(act_h[:, k % 2, LO, :], act_full[:, :], act_h[:, k % 2, HI, :].bitcast(F32),
                                    ALU.subtract).then_inc(dve["D"], 1)
                elif kind == "U":
                    l, b = i
                    n = li[l]
                    v.wait_ge(pe["U"], nth("U", i))
                    for tt in range(TT):
                        v.bn_stats(bn[:, b, tt, :], bank("U", i)[:, tt, :]).then_inc(dve_link, 1)
                        link[0] += 1
                    for tt in range(TT):
                        v.wait_ge(dve_link, link[0] - TT + 1 + 2 * tt if tt == 0 else link[0])
                        v.bn_aggr(mv[:, n, b, tt, :], bn[:, b, tt, :]).then_inc(dve_link, 1)
                        link[0] += 1
                    v.wait_ge(dve_link, link[0])
                    v.tensor_scalar(veps[:, n, b, :], mv[:, n, b, :, 1], LN_EPS, None, ALU.add)\
                        .then_inc(dve["U"], 1)
                elif kind == "N":
                    l, b = i
                    n = li[l]
                    v.wait_ge(pool_rstd, nth("U", i))
                    v.scalar_tensor_tensor(out=nmr[:, n, b, :], in0=mv[:, n, b, :, 0], scalar=-1.0,
                                           in1=rstd[:, n, b, :], op0=ALU.mult, op1=ALU.mult).then_inc(dve["N"], 1)
                elif kind == "T":
                    l, b = i
                    k = nth("T", i)
                    v.wait_ge(act["T"], KF * k)
                    if l == 0 and b >= 2:
                        v.wait_ge(pe["S"], nth("S", b - 2))
                        v.wait_ge(pe["V"], nth("V", b - 2))
                    if l == 2 and b < 2:
                        v.wait_ge(pe["S"], nth("S", b + 2))
                        v.wait_ge(pe["V"], nth("V", b + 2))
                    if l == 2 and b >= 2:
                        v.wait_ge(pe["U"], nth("U", (3, b - 2)))
                    v.tensor_copy(xmid[:, HI, b % 2], layer_out(l, b)[:, :, :]).then_inc(dve["T"], 1)
                    v.wait_ge(dve["T"], 2 * k - 1)
                    v.tensor_tensor(xmid[:, LO, b % 2], layer_out(l, b)[:, :, :], xmid[:, HI, b % 2].bitcast(F32),
                                    ALU.subtract).then_inc(dve["T"], 1)
                elif kind in ("MN", "Y", "V", "PT"):
                    v.wait_ge(act[kind], nth(kind, i))
                    v.tensor_tensor(pair(kind, i, LO), bank(kind, i), pair(kind, i, HI).bitcast(F32),
                                    ALU.subtract).then_inc(dve[kind], 1)
                elif kind == "ROWS":
                    if i == 0:
                        selectors()
                    bias_rows(i)
                elif kind == "CB":
                    cms_biases()
                elif kind == "S":
                    v.wait_ge(pe["S"], nth("S", i))
                    step(v.tensor_reduce(smax[:, i, :], bank("S", i), AX_X, ALU.max))
                    v.tensor_scalar(nmax[:, i, :], smax[:, i, :], -V ** -0.5, None, ALU.mult).then_inc(dve["max"], 1)
                elif kind == "E":
                    v.wait_ge(act["E"], TT * nth("E", i))
                    step(v.reciprocal(rsum[:, i, :], ssum[:, i, :]))
                    for tt in range(TT):
                        v.tensor_scalar(prob[:, tt, :], prob[:, tt, :], rsum[:, i, tt:tt + 1], None, ALU.mult)\
                            .then_inc(dve["E"], 1)
                elif kind == "A":
                    v.wait_ge(act["A"], KF * nth("A", i))
                    for kf in range(KF):
                        v.scalar_tensor_tensor(out=attn_of(i, LO, kf), in0=bank("A", i)[:, kf, :],
                                               scalar=sv[:, BP + kf:BP + kf + 1], in1=attn_of(i, HI, kf).bitcast(F32),
                                               op0=ALU.add, op1=ALU.subtract).then_inc(dve["A"], 1)
                elif kind in ("H1", "H2B"):
                    m = hid(0 if kind == "H1" else 1, *i)
                    v.wait_ge(act["hidden"], 2 * (m + 1))
                    v.tensor_tensor(hidden[:, m % HID_SLOTS, LO, :], hidden_full[:, m % 2, :],
                                    hidden[:, m % HID_SLOTS, HI, :].bitcast(F32), ALU.subtract)\
                        .then_inc(dve["hidden"], 1)
                elif kind == "CE":
                    n = 0
                    for kf in range(KF):
                        n += CB
                        v.wait_ge(act["CE"], CB * KF * i + n)
                        for j in range(CB):
                            b = CB * i + j
                            v.scalar_tensor_tensor(out=cms[:, LO, kf, j * S:(j + 1) * S],
                                                   in0=acc[:, kf, j * S:(j + 1) * S], scalar=cbias[:, kf, b:b + 1],
                                                   in1=cms[:, HI, kf, j * S:(j + 1) * S].bitcast(F32),
                                                   op0=ALU.add, op1=ALU.subtract).then_inc(dve["CE"], 1)
                    for j in range(CB):
                        for kf in range(KF):
                            b = CB * i + j
                            v.scalar_tensor_tensor(out=res[:, b, kf, :], in0=acc[:, kf, j * S:(j + 1) * S],
                                                   scalar=rbias[:, kf, b:b + 1], in1=res[:, b, kf, :],
                                                   op0=ALU.add, op1=ALU.add).then_inc(dve["CE"], 1)
                elif kind == "ME":
                    k = nth("ME", i)
                    j = i % CB
                    v.wait_ge(pe["hidden_used"], hid(1, i // CB, HT - 1) + 1)
                    v.wait_ge(dve["CE"], 2 * CB * KF * (i // CB + 1))
                    v.tensor_tensor(res[:, i], acc[:, :, j * S:(j + 1) * S], res[:, i], ALU.add)\
                        .then_inc(dve["z"], 1)
                    v.wait_ge(dve["z"], k)
                    if i >= 2:
                        v.wait_ge(pe["U"], nth("U", (2, i - 2)))
                    v.tensor_scalar(xin[:, HI, i % 2], res[:, i], 0.0, 1.0, ALU.max, ALU.min)\
                        .then_inc(dve["ME"], 1)
                    v.tensor_scalar(res[:, i], res[:, i], 0.0, 1.0, ALU.max, ALU.min).then_inc(dve["ME"], 1)
                    v.wait_ge(dve["ME"], 3 * k - 1)
                    v.tensor_tensor(xin[:, LO, i % 2], res[:, i], xin[:, HI, i % 2].bitcast(F32), ALU.subtract)\
                        .then_inc(dve["ME"], 1)
                elif kind == "F":
                    l, b = i
                    n = li[l]
                    k = nth("F", i)
                    v.wait_ge(pool_rstd, nth("U", i))
                    v.wait_ge(s_gb[b % 2], 16 * (b // 2 + 2))
                    for tt in range(TT):
                        step(v.scalar_tensor_tensor(out=res[:, b, tt, :], in0=bank("U", i)[:, tt, :],
                                                    scalar=mv[:, n, b, tt, 0:1], in1=gb[:, b % 2, 0, :],
                                                    op0=ALU.subtract, op1=ALU.mult))
                        v.scalar_tensor_tensor(out=res[:, b, tt, :], in0=res[:, b, tt, :],
                                               scalar=rstd[:, n, b, tt:tt + 1], in1=gb[:, b % 2, 1, :],
                                               op0=ALU.mult, op1=ALU.add).then_inc(dve["F"], 1)

        @block.tensor
        def _(t):
            def take(step):
                if before[step]:
                    for s, n in freed(before[step]):
                        t.wait_ge(s, n)

            def products(out, pairs):
                todo = [(lhs(p), rhs(q)) for lhs, rhs in pairs for p, q in PASSES]
                for n, (l, r) in enumerate(todo):
                    ins = t.matmul(out, l, r, start=(n == 0), stop=(n == len(todo) - 1))
                return ins

            for kind, i in ORDER:
                if (kind, i) in bank_of:
                    take((kind, i))
                if kind == "D":
                    l, b = i
                    t.wait_ge(*split_done(("adp", i)))
                    if l == 0:
                        t.wait_ge(*split_done(("x", b)))
                    elif l == 2:
                        t.wait_ge(dve["ME"], 3 * nth("ME", b))
                    else:
                        t.wait_ge(dve["T"], 2 * nth("T", (2, b)))
                    products(bank("D", i)[:, 0, :],
                             [(lambda p, kf=kf: adp[:, p, adp_slot[i], kf * P:(kf + 1) * P],
                               lambda p, kf=kf: layer_in(l, b, p)[:, kf, :]) for kf in range(KF)])\
                        .then_inc(pe["D"], 1)
                elif kind == "U":
                    l, b = i
                    k = nth("D", i)
                    t.wait_ge(dve_rows, b + 1)
                    for tt in range(TT):
                        o = bank("U", i)[:, tt, :]
                        t.matmul(o, ones_row[:, li[l], :], rows[:, b, :], start=True, stop=False)
                        for p in (HI, LO):
                            for kf in range(KF):
                                t.matmul(o[:, kf * P:(kf + 1) * P], layer_in(l, b, p)[:, kf, tt * P:(tt + 1) * P],
                                         ident_r[:, :], start=False, stop=False)
                        if tt == 0:
                            t.wait_ge(dve["D"], k)
                        for n, (p, q) in enumerate(PASSES):
                            ins = t.matmul(o, act_h[:, k % 2, p, tt * P:(tt + 1) * P],
                                           adp[:, q, adp_slot[i], KF * P:KF * P + V],
                                           start=False, stop=(n == len(PASSES) - 1))
                    ins.then_inc(pe["U"], 1)
                elif kind == "T":
                    k = nth("N", i)
                    t.wait_ge(act["N"], TT * k)
                    for kf in range(KF):
                        for tt in range(TT):
                            ins = t.transpose(bank("T", i)[:, kf, tt * P:(tt + 1) * P],
                                              yn[:, k % 2, tt, kf * P:(kf + 1) * P], ident)
                    ins.then_inc(pe["T"], 1)
                elif kind == "MN":
                    for j in (2 * i, 2 * i + 1):
                        t.wait_ge(*split_done(("mn", j)))
                    for it in range(KF):
                        ins = products(bank("MN", i)[:, it, :],
                                       [(lambda p, kd=kd: w4[:, p, 4 * i + kd, it * P:(it + 1) * P],
                                         lambda p, kd=kd: w4[:, p, 4 * i + 2 + kd, :]) for kd in range(KF)])
                    ins.then_inc(pe["MN"], 1)
                elif kind == "Y":
                    b = i
                    t.wait_ge(dve["T"], 2 * nth("T", (0, b)))
                    t.wait_ge(dve["MN"], 1)
                    for jt in range(KF):
                        ins = products(bank("Y", i)[:, jt, :],
                                       [(lambda p, kf=kf: mn[:, p, 0, kf, jt * P:(jt + 1) * P],
                                         lambda p, kf=kf: xmid[:, p, b % 2, kf, :]) for kf in range(KF)])
                    ins.then_inc(pe["Y"], 1)
                elif kind == "V":
                    b = i
                    t.wait_ge(dve["MN"], 2)
                    for tt in range(TT):
                        ins = products(bank("V", i)[:, tt, :],
                                       [(lambda p, kf=kf: xmid[:, p, b % 2, kf, tt * P:(tt + 1) * P],
                                         lambda p, kf=kf: mn[:, p, 1, kf, :]) for kf in range(KF)])
                    ins.then_inc(pe["V"], 1)
                elif kind == "S":
                    b = i
                    t.wait_ge(dve["Y"], nth("Y", i))
                    for tt in range(TT):
                        ins = products(bank("S", i)[:, tt, :],
                                       [(lambda p, kf=kf: qk[:, p, kf, tt * P:(tt + 1) * P],
                                         lambda p, kf=kf: xmid[:, p, b % 2, kf, :]) for kf in range(KF)])
                    ins.then_inc(pe["S"], 1)
                elif kind == "PT":
                    t.wait_ge(dve["E"], TT * nth("E", i))
                    for ts in range(TT):
                        for tt in range(TT):
                            ins = t.transpose(bank("PT", i)[:, ts, tt * P:(tt + 1) * P],
                                              prob[:, tt, ts * P:(ts + 1) * P], ident)
                    ins.then_inc(pe["PT"], 1)
                elif kind == "A":
                    b = i
                    t.wait_ge(dve["PT"], nth("PT", i))
                    t.wait_ge(dve["V"], nth("V", i))
                    for jt in range(KF):
                        ins = products(bank("A", i)[:, jt, :],
                                       [(lambda p, ts=ts: vv[:, p, b % 2, ts, jt * P:(jt + 1) * P],
                                         lambda p, ts=ts: probT[:, p, ts, :]) for ts in range(TT)])
                    ins.then_inc(pe["A"], 1)
                elif kind == "H1":
                    c, ht = i
                    t.wait_ge(*split_done(("w", ht // 2)))
                    if ht == 0:
                        t.wait_ge(dve["A"], KF * nth("A", CB * c + CB - 1))
                    products(ring[bank_of[(kind, i)]][:, :],
                             [(lambda p, kf=kf: w1[:, p, ht, kf, :],
                               lambda p, kf=kf: attn[:, c, p, kf, :]) for kf in range(KF)])\
                        .then_inc(pe["hidden"], 1)
                elif kind == "H2A":
                    c, ht = i
                    t.wait_ge(*split_done(("w", 8 + ht)))
                    o = ring[bank_of[(kind, i)]][:, :]
                    n = 0
                    for kf in range(KF):
                        for p, q in PASSES:
                            t.matmul(o, w3[:, p, ht, kf, :], attn[:, c, q, kf, :], start=(n == 0), stop=False)
                            n += 1
                elif kind == "H2B":
                    c, ht = i
                    if ht == 0:
                        t.wait_ge(dve["CE"], 2 * CB * KF * c + CB * KF)
                    o = ring[bank_of[("H2A", i)]][:, :]
                    n = 0
                    for kf in range(KF):
                        for p, q in PASSES:
                            ins = t.matmul(o, w3[:, p, ht, KF + kf, :], cms[:, q, kf, :], start=False,
                                           stop=(n == KF * len(PASSES) - 1))
                            n += 1
                    ins.then_inc(pe["hidden"], 1)
                elif kind in ("CMS", "MOD"):
                    c, ht = i
                    phase = 0 if kind == "CMS" else 1
                    w, m = (w4 if phase else w2), hid(phase, c, ht)
                    t.wait_ge(*split_done(("w", (16 if phase else 4) + ht // 2)))
                    t.wait_ge(dve["hidden"], m + 1)
                    if ht == 0 and phase == 1:
                        t.wait_ge(dve["CE"], 2 * CB * KF * (c + 1))
                    if ht == 0 and phase == 0 and c >= 1:
                        t.wait_ge(dve["z"], nth("ME", CB * c - 1))
                    for ft in range(KF):
                        for n, (p, q) in enumerate(PASSES):
                            ins = t.matmul(acc[:, ft, :], w[:, p, ht, ft * P:(ft + 1) * P],
                                           hidden[:, m % HID_SLOTS, q, :], start=(ht == 0 and n == 0),
                                           stop=(ht == HT - 1 and n == len(PASSES) - 1))
                    ins.then_inc(pe["hidden_used"], 1)



def kernel(**inputs):
    import numpy as np
    import concourse.bacc as bacc
    from concourse.bass_utils import run_bass_kernel_spmd as run

    a = {k: np.asarray(v) for k, v in inputs.items()}
    out_shape = a["x"].shape

    def tiles(w):
        return w.reshape(w.shape[0] // P, P, w.shape[1]).transpose(1, 0, 2)

    def columns(*vecs):
        return np.concatenate([u.reshape(-1, P).T for u in vecs], axis=1)

    def cut(w):
        return w.reshape(P, -1, PIECE).transpose(1, 0, 2)

    def hidden_tiles(w):
        k, h = w.shape
        return w.reshape(k // P, P, h // P, P).transpose(1, 2, 0, 3).reshape(P, -1)

    weights = np.concatenate([
        np.stack([tiles(a["L1_cond_" + n].T if n != "Wp" else a["L1_cond_Wp"]).reshape(P, PIECE)
                  for n in ("Wq", "Wk", "Wv", "Wp")]),
        cut(hidden_tiles(a["L1_cond_cW1"])), cut(tiles(a["L1_cond_cW2"]).reshape(P, -1)),
        cut(hidden_tiles(a["L1_cond_mW1"])), cut(tiles(a["L1_cond_mW2"]).reshape(P, -1))])
    adapters = np.stack([
        np.concatenate([tiles(a[f"L{l}_cond_W_down"][e]).reshape(P, -1), a[f"L{l}_cond_W_up"][e]], axis=1)
        for l in LAYERS for e in range(E)])
    adapters0 = np.stack([np.concatenate([adapters[e], columns(
        a["L0_cond_b_down"][e], a["L0_cond_gamma"][e], a["L0_cond_beta"][e],
        a["L2_cond_b_down"][e], a["L2_cond_ln_w"][e], a["L2_cond_ln_b"][e],
        a["L3_cond_b_down"][e])], axis=1) for e in range(E)])
    expert_rows = np.concatenate([a["L0_cond_b_up"], a["L2_cond_b_up"], a["L3_cond_b_up"],
                                  a["L3_cond_gamma"], a["L3_cond_beta"]], axis=1)
    vecs = columns(*(a["L1_cond_" + n] for n in ("cb1", "mb1", "bp", "cb2", "mb2")))
    xs = a["x"].transpose(0, 2, 1).reshape(B, KF, P, S).transpose(0, 2, 1, 3).reshape(B, P, KF * S)
    arrays = {
        "roles": a["itok_B_1_2"].reshape(1, B), "codes": a["itok_B_17_1546"].reshape(1, B),
        "xs": xs, "weights": weights, "adapters0": adapters0, "adapters": adapters[E:],
        "expert_rows": expert_rows, "vecs": vecs}
    arrays = {f"in_{k}": np.ascontiguousarray(v) for k, v in arrays.items()}

    nc = bacc.Bacc("TRN2", target_bir_lowering=False, num_devices=1, dynamic_dma_scratch_size=1024)
    args = [nc.dram_tensor(k, v.shape, mybir.dt.from_np(v.dtype), kind="ExternalInput").ap()
            for k, v in arrays.items()]
    out = nc.dram_tensor("out_x", out_shape, F32, kind="ExternalOutput").ap()
    build(nc, *args, out)
    r = run(nc, [arrays], core_ids=[0])
    return r.results[0]["out_x"]
```

```python
from contextlib import ExitStack

import concourse.bass as bass
from concourse import mybir

P = 128
F32 = mybir.dt.float32
F32R = mybir.dt.float32r
I32 = mybir.dt.int32
ALU = mybir.AluOpType
ACT = mybir.ActivationFunctionType
AX_X = mybir.AxisListType.X

B, S, V = 4, 256, 256
KF = V // P
TT = S // P
CB = 2
NC = B // CB
CT = CB * S
HT = 4 * V // P
E = 3
LN_EPS = 1e-5
HI, LO = 0, 1
LO_ROW = 32
PASSES = ((HI, HI), (HI, LO), (LO, HI))
PIECE = 512
RAW_SLOTS = 6
ADP_SLOTS = 4
HID_SLOTS = 3
RING = 6
LAYERS = (0, 2, 3)

BD = {0: 0, 2: 5, 3: 10}
GAMMA = {0: 1, 2: 6}
BETA = {0: 3, 2: 8}
EV = 11
CB1, MB1, BP, CB2, MB2 = 0, HT, 2 * HT, 2 * HT + KF, 2 * HT + 2 * KF
SV = 2 * HT + 3 * KF


SCHEDULE = """
# L0 and the attention of sequences 0, 1 and 2
x.0 adp.00 ROWS.0 x.1 adp.01 ROWS.1 WARM.12 D.00 w.0 mn.1 WARM.4 D.01 U.00 x.2 mn.0 adp.02 mn.2 mn.3 w.1
N.00 ROWS.2 U.01 D.02 MN.0 w.2 T.00 N.01 U.02 MN.1 w.4 w.3 T.01 Y.0 N.02 w.5 V.0 S.0 E.0 Y.1 T.02 w.7
PT.0 S.1 E.1 V.1 Y.2 w.6 x.3 adp.03 ROWS.3 w.8 A.0 w.9 PT.1 S.2 V.2 E.2 w.11 A.1 D.03 w.10 PT.2 w.12
CB.0
# cms of chunk 0, and the rest of sequences 2 and 3
H1.00 w.13 w.14 w.15 H1.01 w.16 A.2 H1.02 H1.03 w.17 CMS.00 w.18 w.19 adp.30 CMS.01 U.03 adp.20 H1.04
adp.21 adp.31 CMS.02 H1.05 CMS.03 N.03 H1.06 CMS.04 H1.07 CMS.05 T.03
# the modifier of chunk 0
H2A.00 CMS.06 CMS.07 H2A.01 CE.0 Y.3 H2A.02 H2A.03 H2B.00 S.3 E.3 V.3 H2B.01 H2A.04 H2B.02 MOD.00 H2A.05
PT.3 H2B.03 MOD.01 H2A.06 H2B.04 MOD.02 H2A.07 A.3 H2B.05 MOD.03 H2B.06 MOD.04 H2B.07 MOD.05
# cms of chunk 1, and L2 of chunk 0
H1.10 MOD.06 H1.11 MOD.07 Z.00 Z.10 Z.01 Z.11 ME.00 ME.10 ME.01 ME.11 H1.12 H1.13 CMS.10 CMS.11 D.20
H1.14 CMS.12 U.20 H1.15 CMS.13 D.21 H1.16 CMS.14 N.20 H1.17 CMS.15 U.21 CMS.16 T.20 H2A.11 adp.32 CMS.17
# the modifier of chunk 1, and L2 and L3 of chunk 0
CE.1 N.21 adp.22 H2A.10 H2A.12 H2A.13 D.30 H2B.10 T.21 adp.23 H2B.11 H2A.14 U.30 adp.33 H2B.12 MOD.10
H2A.15 D.31 H2B.13 MOD.11 H2A.16 F.30 H2B.14 MOD.12 H2A.17 U.31 H2B.15 MOD.13 F.31 H2B.16 MOD.14 H2B.17
MOD.15 END.0 Z.20 ME.20 Z.30 END.1 Z.21 ME.21 ME.30 Z.31 ME.31
# L2 and L3 of chunk 1
WARM.8 D.22 U.22 D.23 N.22 U.23 T.22 N.23 WARM.6 D.32 T.23 U.32 D.33 F.32 U.33 F.33
"""


def splitter(piece):
    kind, i = piece
    if (kind == "x" and i != 1) or (kind == "adp" and i[0] == 0) or (kind == "mn" and i >= 2):
        return "AV"
    return "P"


def order():
    steps = []
    for line in SCHEDULE.splitlines():
        for word in line.split("#")[0].split():
            kind, digits = word.split(".")
            one = kind in ("x", "mn", "w", "ROWS", "MN", "Y", "S", "E", "V", "PT", "A", "CB", "CE", "END", "WARM")
            i = int(digits) if one else tuple(int(c) for c in digits)
            if kind == "WARM":
                i = (len(steps), i)
            steps.append(("W", (kind, i)) if kind in ("x", "adp", "mn", "w") else (kind, i))
    assert len(set(steps)) == len(steps)
    return steps


def build(nc, roles, codes, xs, weights, adapters0, adapters, expert_rows, vecs, out):
    ORDER = order()
    PIECES = [(*i, splitter(i)) for kind, i in ORDER if kind == "W"]
    nth_of, seen = {}, {}
    for kind, i in ORDER:
        seen[kind] = seen.get(kind, 0) + 1
        nth_of[(kind, i)] = seen[kind]

    def nth(kind, i):
        return nth_of[(kind, i)]

    def wide(i):
        return i[0] != 0 and i[1] >= B - CB

    needed_until = {"U": ("N", "F"), "S": ("E",), "H2A": ("H2B",)}
    where = {step: n for n, step in enumerate(ORDER)}
    bank_of, before = {}, {}
    last, free_at = [None] * RING, [n - RING for n in range(RING)]
    for n, (kind, i) in enumerate(ORDER):
        if kind in ("WARM", "D", "U", "T", "MN", "Y", "V", "S", "PT", "A", "H1", "H2A"):
            for part in range(TT if kind == "U" and wide(i) else 1):
                k = min(range(RING), key=lambda m: free_at[m])
                assert free_at[k] < n
                bank_of[(kind, i, part)], before[(kind, i, part)] = k, last[k]
                last[k] = (kind, i, part)
                free_at[k] = next(where[(q, i)] for q in needed_until.get(kind, (kind,)) if (q, i) in where)

    def hid(phase, c, ht):
        return (c * 2 + phase) * HT + ht

    place_of, place_before, landing = {}, {}, {}
    users, n = {}, 0
    for kind, i, who in PIECES:
        if kind == "x":
            place = ("res", i)
        elif kind == "mn" and i >= 2:
            place = ("gb", i - 2)
        else:
            place = ("raw", n % RAW_SLOTS)
            n += 1
        place_of[(kind, i)] = place
        before_it = users.setdefault(place, [])
        place_before[(kind, i)] = before_it[-1] if before_it else None
        before_it.append((kind, i))
        landing[(kind, i)] = 16 * len(before_it)
    counts = {"AV": 0, "P": 0}
    split_count = {}
    who_of = {(k, i): w for k, i, w in PIECES}
    for kind, i in ORDER:
        if kind == "W":
            counts[who_of[i]] += 1
            split_count[i] = counts[who_of[i]]
    adp_pieces = [i for k, i, _ in PIECES if k == "adp"]
    adp_slot = {i: n % ADP_SLOTS for n, i in enumerate(adp_pieces)}
    adp_before = {i: (adp_pieces[n - ADP_SLOTS] if n >= ADP_SLOTS else None) for n, i in enumerate(adp_pieces)}

    with ExitStack() as ctx:
        def sb(name, shape, dt=F32):
            return ctx.enter_context(nc.sbuf_tensor(name, shape, dt))

        def sem(name):
            return ctx.enter_context(nc.semaphore(name))

        raw = sb("raw", [P, RAW_SLOTS, PIECE + EV])
        w1 = sb("w1", [P, 2, HT, KF, P], F32R)
        w2 = sb("w2", [P, 2, HT, V], F32R)
        w3 = sb("w3", [P, 2, HT, 2 * KF, P], F32R)
        w4 = sb("w4", [P, 2, HT, V], F32R)
        adp = sb("adp", [P, 2, ADP_SLOTS, PIECE], F32R)
        mn = sb("mn", [P, 2, 2, KF, V], F32R)
        xin = sb("xin", [P, 2, 2, KF, S], F32R)
        xmid = sb("xmid", [P, 2, 2, KF, S], F32R)
        res = sb("res", [P, B, KF, S])
        qk = sb("qk", [P, 2, KF, S], F32R)
        vv = sb("vv", [P, 2, 2, TT, V], F32R)
        prob = sb("prob", [P, TT, S])
        probT = sb("probT", [P, 2, TT, S], F32R)
        attn = sb("attn", [P, NC, 2, KF, CT], F32R)
        hidden = sb("hidden", [P, HID_SLOTS, 2, CT], F32R)
        hidden_full = sb("hidden_full", [P, 2, CT])
        cms = sb("cms", [P, 2, KF, CT], F32R)
        act_h = sb("act_h", [P, 2, 2, S], F32R)
        act_full = sb("act_full", [P, S])
        yn = sb("yn", [P, 2, TT, V])
        full = sb("full", [P, KF, S])
        gb = sb("gb", [P, 2, 2, V])
        rows = sb("rows", [P, B, V], F32R)
        ones_row = sb("ones_row", [P, 3, P], F32R)
        ident_r = sb("ident_r", [P, P], F32R)
        ident = ident_r[:, :].bitcast(F32)
        ev = sb("ev", [P, B, EV])
        sv = sb("sv", [P, SV])
        code_i = sb("code_i", [P, B], I32)
        code_f = sb("code_f", [P, B])
        feat_i = sb("feat_i", [P, KF], I32)
        feat_f = sb("feat_f", [P, KF])
        cbias = sb("cbias", [P, KF, B])
        rbias = sb("rbias", [P, KF, B])
        bn = sb("bn", [P, B, TT, 6])
        mv = sb("mv", [P, 3, B, TT, 2])
        veps = sb("veps", [P, 3, B, TT])
        rstd = sb("rstd", [P, 3, B, TT])
        nmr = sb("nmr", [P, 3, B, TT])
        mhalf = sb("mhalf", [P, TT])
        smax = sb("smax", [P, B, TT])
        nmax = sb("nmax", [P, B, TT])
        ssum = sb("ssum", [P, B, TT])
        rsum = sb("rsum", [P, B, TT])

        ring = [ctx.enter_context(nc.psum_tensor(f"ring{i}", [P, 512], F32)) for i in range(RING)]
        acc = ctx.enter_context(nc.psum_tensor("acc", [P, KF, CT], F32))

        def bank(kind, i):
            return ring[bank_of[(kind, i, 0)]][:, :].rearrange("p (a b) -> p a b", a=2)

        def up(i, tt):
            return ring[bank_of[("U", i, tt)]][:, 0:V] if wide(i) else bank("U", i)[:, tt, :]

        s_raw = [sem(f"raw_landed{i}") for i in range(RAW_SLOTS)]
        s_vec, s_code = sem("vecs_landed"), sem("codes_landed")
        s_rows = [sem(f"rows_landed{b}") for b in range(B)]
        s_x = [sem(f"x_landed{b}") for b in range(B)]
        s_gb = [sem(f"gamma_beta_landed{i}") for i in range(2)]
        s_out = sem("out_landed")
        act_w, dve_w, pool_hi, pool_w = sem("act_W_hi"), sem("dve_W_lo"), sem("pool_W_hi"), sem("pool_W_lo")
        pool_zero, pool_const = sem("pool_zeros"), sem("pool_constants")
        dve_const, dve_rows, dve_link = sem("dve_constants"), sem("dve_rows"), sem("dve_link")
        pe = {k: sem(f"pe_{k}") for k in ("D", "U", "T", "MN", "Y", "V", "S", "PT", "A", "hidden", "hidden_used", "end", "U0")}
        act = {k: sem(f"act_{k}") for k in ("D", "N", "T", "MN", "Y", "V", "E", "PT", "A", "hidden", "CE")}
        dve = {k: sem(f"dve_{k}") for k in
               ("D", "U", "N", "T", "MN", "Y", "V", "max", "E", "PT", "A", "hidden", "CE", "z", "ME", "F", "wide_rows", "centred")}
        dve_var = sem("dve_variance")
        dve_me_lo, pool_me = sem("dve_ME_lo"), sem("pool_ME_lo")
        pool_rstd, act_first = sem("pool_rstd"), sem("act_first_gelu")

        def freed(step):
            kind, i, part = step
            k = nth(kind, i)
            if kind == "WARM":
                return []
            if kind == "D":
                return [(act["D"], 2 * k)]
            if kind == "U":
                if i[0] == 3:
                    return [(dve["F"], TT * nth("F", i))]
                return [rows_done(i, part if wide(i) else TT - 1)]
            if kind == "T":
                return [(act["T"], KF * k)]
            if kind == "S":
                return [(act["E"], TT * k)]
            if kind in ("MN", "Y", "V", "PT"):
                return [(dve[kind], k)]
            if kind == "A":
                return [(dve["A"], KF * k)]
            m = hid(0 if kind == "H1" else 1, *i)
            return [(act["hidden"], 2 * (m + 1))]

        def rows_done(i, tt):
            narrow = sum(kind == "N" and not wide(j) for kind, j in ORDER)
            if not wide(i):
                return act["N"], TT * (nth("N", i) - 1) + tt + 1
            n = nth("N", i) - narrow
            return (dve["wide_rows"], n) if tt else (act["N"], TT * narrow + n)

        def me_count(b, kf):
            return 2 * nth("ME", (b, kf))

        def split_done(piece):
            return (dve_w if who_of[piece] == "AV" else pool_w), split_count[piece]

        def source(piece):
            where, n = place_of[piece]
            if where == "res":
                return res[:, n]
            if where == "gb":
                return gb[:, n].rearrange("p a b -> p (a b)")
            return raw[:, n, 0:PIECE]

        def landed(piece):
            where, n = place_of[piece]
            return {"res": s_x, "gb": s_gb, "raw": s_raw}[where][n], landing[piece]

        def split_target(piece, part):
            kind, i = piece
            if kind == "x":
                return layer_in(0, i, part)
            if kind == "adp":
                return adp[:, part, adp_slot[i], :]
            if kind == "mn":
                return w4[:, part, 2 * i:2 * i + 2, :].rearrange("p a b -> p (a b)")
            if i < 4:
                return w1[:, part, 2 * i:2 * i + 2, :, :].rearrange("p a b c -> p (a b c)")
            if i < 8:
                return w2[:, part, 2 * (i - 4):2 * (i - 4) + 2, :].rearrange("p a b -> p (a b)")
            if i < 16:
                return w3[:, part, i - 8, :, :].rearrange("p a b -> p (a b)")
            return w4[:, part, 2 * (i - 16):2 * (i - 16) + 2, :].rearrange("p a b -> p (a b)")

        def target_free(piece):
            kind, i = piece
            if kind == "adp" and adp_before[i]:
                return [(pe["U"], nth("U", adp_before[i]))]
            if kind == "w" and i >= 16:
                return [(pe["MN"], 2)]
            return []

        def layer_in(l, b, part):
            if l == 0 and b >= CB:
                return attn[:, 1, part, :, (b - CB) * S:(b - CB + 1) * S]
            return (xmid if l == 3 else xin)[:, part, b % 2]

        def attn_of(b, part, kf):
            return attn[:, b // CB, part, kf, (b % CB) * S:(b % CB + 1) * S]

        def pair(kind, i, part):
            return {"MN": mn[:, part, i % 2], "Y": qk[:, part], "V": vv[:, part, i % 2],
                    "PT": probT[:, part]}[kind]

        def layer_out(l, b):
            return res[:, b] if l == 0 else full

        def landed_rows(b):
            return hidden_full[0:3, b // 2, (b % 2) * V:(b % 2 + 1) * V]

        li = {l: n for n, l in enumerate(LAYERS)}
        block = ctx.enter_context(nc.Block())

        @block.sync
        def _(sp):
            role = {}

            def load(kind, i):
                piece = (kind, i)
                if place_before[piece]:
                    sp.wait_ge(*split_done(place_before[piece]))
                if kind == "adp":
                    l, b = i
                    if b not in role:
                        role[b] = sp.value_load(roles[0:1, b:b + 1], min_val=0, max_val=E - 1)
                    if l == 0:
                        dst = raw[:, place_of[piece][1], :]
                        src = adapters0[bass.ds(role[b], 1), :, :].rearrange("o p n -> p (o n)")
                    else:
                        dst = source(piece)
                        src = adapters[bass.ds(role[b] + E * (li[l] - 1), 1), :, :].rearrange("o p n -> p (o n)")
                else:
                    dst = source(piece)
                    src = weights[{"mn": 0, "w": 4}[kind] + i, :, :]
                s, _ = landed(piece)
                sp.dma_start(dst, src).then_inc(s, 16)

            def gamma_beta(b):
                if b >= 2:
                    sp.wait_ge(dve["F"], 2 * nth("F", (3, b - 2)))
                else:
                    sp.wait_ge(*split_done(("mn", 2 + b)))
                sp.dma_start(gb[:, b % 2, :, :].rearrange("p a v -> p (a v)"),
                             expert_rows[bass.ds(role[b], 1), 3 * V:5 * V].partition_broadcast(P)
                             .rearrange("p o n -> p (o n)")).then_inc(s_gb[b % 2], 16)

            def load_rows(b):
                sp.dma_start(landed_rows(b), expert_rows[bass.ds(role[b], 1), 0:3 * V]
                             .rearrange("o (l n) -> (o l) n", l=3)).then_inc(s_rows[b], 16)

            first = [("adp", (0, 0)), ("adp", (0, 1))]
            rest = [(kind, i) for kind, i, _ in PIECES if (kind, i) not in first + [("x", 0), ("x", 1)]]
            for piece in first + rest:
                if piece[0] == "x":
                    sp.dma_start(source(piece), xs[piece[1], :, :].rearrange("p (a b) -> p a b", a=KF))\
                        .then_inc(landed(piece)[0], 16)
                else:
                    load(*piece)
                if piece[0] == "adp" and piece[1][0] == 0:
                    load_rows(piece[1][1])
                if piece == ("mn", 3):
                    sp.dma_start(sv[:, :], vecs).then_inc(s_vec, 16)
                    sp.dma_start(code_i[:, :], codes.partition_broadcast(P).rearrange("p o n -> p (o n)"))\
                        .then_inc(s_code, 16)
                if piece == ("w", 16):
                    gamma_beta(0)
                    gamma_beta(1)
            for kind, i in ORDER:
                if kind != "F":
                    continue
                b = i[1]
                for tt in range(TT):
                    sp.wait_ge(dve["F"], TT * (nth("F", i) - 1) + tt + 1)
                    sp.dma_start(out[b, tt * P:(tt + 1) * P, :], res[:, b, tt, :]).then_inc(s_out, 16)
                if b < 2:
                    gamma_beta(b + 2)
            sp.wait_ge(s_out, 16 * B * TT)

        @block.gpsimd
        def _(pool):
            eye = yn[:, 1, 0, 0:P]
            pool.memset(eye, 0.0).then_inc(pool_zero, 1)
            pool.wait_ge(pool_zero, 1)
            pool.affine_select(out=eye, in_=eye, compare_op=ALU.not_equal, fill=1.0, base=0,
                               pattern=[[-1, P]], channel_multiplier=1).then_inc(pool_const, 1)
            pool.memset(hidden[:, 0, HI, :].bitcast(F32), 0.0).then_inc(pool_zero, 1)
            pool.memset(mhalf[:, :], -0.5).then_inc(pool_const, 1)
            pool.iota(feat_i[:, :], pattern=[[P, KF]], base=0, channel_multiplier=1).then_inc(pool_const, 1)
            for kind, i in ORDER:
                if kind == "W" and who_of[i] == "P":
                    pool.wait_ge(*landed(i))
                    for s, v in target_free(i):
                        pool.wait_ge(s, v)
                    pool.tensor_scalar(split_target(i, HI), source(i), 1.0, 0.0, ALU.mult, ALU.add)\
                        .then_inc(pool_hi, 1)
                    pool.wait_ge(pool_hi, split_count[i])
                    pool.tensor_tensor(split_target(i, LO), source(i), split_target(i, HI).bitcast(F32),
                                       ALU.subtract).then_inc(pool_w, 1)
                if kind == "ME" and i[0] % 2 == 1:
                    b, kf = i
                    pool.wait_ge(dve["ME"], me_count(b, kf))
                    pool.tensor_tensor(xin[:, LO, 1, kf, :], res[:, b, kf, :], xin[:, HI, 1, kf, :].bitcast(F32),
                                       ALU.subtract).then_inc(pool_me, 1)
                if kind == "U":
                    n = li[i[0]]
                    pool.wait_ge(dve["U"], nth("U", i))
                    pool.tensor_tensor(rstd[:, n, i[1], :], veps[:, n, i[1], :], mhalf[:, :], ALU.pow)\
                        .then_inc(pool_rstd, 1)

        @block.scalar
        def _(a):
            def load_x(b):
                a.dma_start(res[:, b].rearrange("p a b -> p (a b)"), xs[b, :, :]).then_inc(s_x[b], 16)

            load_x(0)
            load_x(1)

            a.wait_ge(dve_const, 1)
            a.activation(ssum[:, 0, :], nmax[:, 0, :], ACT.Gelu).then_inc(act_first, 1)

            def gelu_pair(hi, whole, src, bias, done):
                a.activation(hi, src, ACT.Gelu, bias=bias).then_inc(done, 1)
                a.activation(whole, src, ACT.Gelu, bias=bias).then_inc(done, 1)

            for kind, i in ORDER:
                if kind == "W" and who_of[i] == "AV":
                    a.wait_ge(*landed(i))
                    for s, v in target_free(i):
                        a.wait_ge(s, v)
                    a.activation(split_target(i, HI), source(i), ACT.Copy).then_inc(act_w, 1)
                elif kind == "D":
                    l, b = i
                    k = nth("D", i)
                    a.wait_ge(pe["D"], k)
                    if k >= 2:
                        a.wait_ge(dve["D"], k - 1)
                    if k >= 3:
                        a.wait_ge(pe["U"], k - 2)
                    gelu_pair(act_h[:, k % 2, HI, :], act_full[:, :], bank("D", i)[:, 0, :],
                              ev[:, b, BD[l]:BD[l] + 1], act["D"])
                elif kind == "N":
                    l, b = i
                    k = nth("N", i)
                    a.wait_ge(dve["N"], k)
                    if k >= 3:
                        a.wait_ge(pe["T"], k - 2)
                    for tt in range(1 if wide(i) else TT):
                        a.activation(yn[:, k % 2, tt, :], up(i, tt), ACT.Identity,
                                     scale=rstd[:, li[l], b, tt:tt + 1], bias=nmr[:, li[l], b, tt:tt + 1])\
                            .then_inc(act["N"], 1)
                elif kind == "T":
                    l, b = i
                    k = nth("T", i)
                    a.wait_ge(pe["T"], k)
                    if l == 2 and k > B + 1:
                        a.wait_ge(dve["T"], 2 * KF * (k - 1))
                    for kf in range(KF):
                        a.activation(layer_out(l, b)[:, kf, :], bank("T", i)[:, kf, :], ACT.Identity,
                                     scale=ev[:, b, GAMMA[l] + kf:GAMMA[l] + kf + 1],
                                     bias=ev[:, b, BETA[l] + kf:BETA[l] + kf + 1]).then_inc(act["T"], 1)
                elif kind in ("MN", "Y", "V", "PT"):
                    k = nth(kind, i)
                    a.wait_ge(pe[kind], k)
                    if kind == "Y" and k >= 2:
                        a.wait_ge(pe["S"], k - 1)
                    if kind == "PT" and k >= 2:
                        a.wait_ge(pe["A"], k - 1)
                    if kind == "V" and k >= 3:
                        a.wait_ge(pe["A"], k - 2)
                    a.activation(pair(kind, i, HI), bank(kind, i), ACT.Copy).then_inc(act[kind], 1)
                elif kind == "E":
                    k = nth("E", i)
                    a.wait_ge(dve["max"], k)
                    if k >= 2:
                        a.wait_ge(pe["PT"], k - 1)
                    for tt in range(TT):
                        a.activation(prob[:, tt, :], bank("S", i)[:, tt, :], ACT.Exp, bias=nmax[:, i, tt:tt + 1],
                                     scale=V ** -0.5, accum_out=ssum[:, i, tt:tt + 1]).then_inc(act["E"], 1)
                elif kind == "A":
                    if nth("A", i) == 1:
                        a.wait_ge(s_vec, 16)
                    a.wait_ge(pe["A"], nth("A", i))
                    for kf in range(KF):
                        a.activation(attn_of(i, HI, kf), bank("A", i)[:, kf, :], ACT.Identity,
                                     bias=sv[:, BP + kf:BP + kf + 1]).then_inc(act["A"], 1)
                elif kind in ("H1", "H2B"):
                    phase = 0 if kind == "H1" else 1
                    m = hid(phase, *i)
                    a.wait_ge(pe["hidden"], m + 1)
                    if m >= HID_SLOTS:
                        a.wait_ge(pe["hidden_used"], m + 1 - HID_SLOTS)
                    if m >= 2:
                        a.wait_ge(dve["hidden"], m - 1)
                    src = ring[bank_of[("H1" if phase == 0 else "H2A", i, 0)]][:, :]
                    bias = (MB1 if phase else CB1) + i[1]
                    gelu_pair(hidden[:, m % HID_SLOTS, HI, :], hidden_full[:, m % 2, :], src,
                              sv[:, bias:bias + 1], act["hidden"])
                elif kind == "CE":
                    a.wait_ge(pe["hidden_used"], hid(0, i, HT - 1) + 1)
                    if i >= 1:
                        a.wait_ge(pe["hidden"], hid(1, i - 1, HT - 1) + 1)
                    if i == 0:
                        a.wait_ge(dve_const, 6)
                    for kf in range(KF):
                        for j in range(CB):
                            a.activation(cms[:, HI, kf, j * S:(j + 1) * S], acc[:, kf, j * S:(j + 1) * S],
                                         ACT.Identity, bias=cbias[:, kf, CB * i + j:CB * i + j + 1])\
                                .then_inc(act["CE"], 1)

        @block.vector
        def _(v):
            link = [0]

            def step(ins):
                link[0] += 1
                ins.then_inc(dve_link, 1)
                v.wait_ge(dve_link, link[0])

            step(v.memset(rows[:, :, :].bitcast(F32), 0.0))
            v.memset(nmax[:, 0, :], 0.0).then_inc(dve_const, 1)
            def selectors():
                v.wait_ge(pool_const, 3)
                v.tensor_copy(ident_r[:, :], yn[:, 1, 0, 0:P]).then_inc(dve_const, 1)
                for l in range(3):
                    v.tensor_scalar(ones_row[:, l, :], rows[:, B - 1, 0:P].bitcast(F32), yn[:, 1, 0, l:l + 1],
                                    yn[:, 1, 0, LO_ROW + l:LO_ROW + l + 1], ALU.add, ALU.add).then_inc(dve_const, 1)

            def bias_rows(b):
                v.wait_ge(s_rows[b], 16)
                step(v.tensor_copy(rows[0:3, b, :], landed_rows(b)))
                v.tensor_tensor(rows[LO_ROW:LO_ROW + 3, b, :], landed_rows(b), rows[0:3, b, :].bitcast(F32),
                                ALU.subtract).then_inc(dve_rows, 1)

            def cms_biases():
                v.wait_ge(s_code, 16)
                v.wait_ge(s_vec, 16)
                step(v.tensor_copy(code_f[:, :], code_i[:, :]))
                step(v.tensor_copy(feat_f[:, :], feat_i[:, :]))
                for kf in range(KF):
                    step(v.tensor_scalar(cbias[:, kf, :], code_f[:, :], feat_f[:, kf:kf + 1],
                                         sv[:, CB2 + kf:CB2 + kf + 1], ALU.is_equal, ALU.add))
                    ins = v.tensor_scalar(rbias[:, kf, :], cbias[:, kf, :], sv[:, MB2 + kf:MB2 + kf + 1], None, ALU.add)
                    if kf == 0:
                        step(ins)
                ins.then_inc(dve_const, 1)

            for kind, i in ORDER:
                if kind == "W" and who_of[i] == "AV":
                    v.wait_ge(act_w, split_count[i])
                    if i[0] == "adp":
                        step(v.tensor_copy(ev[:, i[1][1], :], raw[:, place_of[i][1], PIECE:PIECE + EV]))
                    v.tensor_tensor(split_target(i, LO), source(i), split_target(i, HI).bitcast(F32),
                                    ALU.subtract).then_inc(dve_w, 1)
                elif kind == "D":
                    k = nth("D", i)
                    v.wait_ge(act["D"], 2 * k)
                    v.tensor_tensor(act_h[:, k % 2, LO, :], act_full[:, :], act_h[:, k % 2, HI, :].bitcast(F32),
                                    ALU.subtract).then_inc(dve["D"], 1)
                elif kind == "U":
                    l, b = i
                    n = li[l]
                    if wide(i):
                        v.wait_ge(pe["U0"], sum(map(wide, (j for q, j in ORDER[:where[(kind, i)] + 1] if q == "U"))))
                    else:
                        v.wait_ge(pe["U"], nth("U", i))
                    for tt in range(TT):
                        if wide(i) and tt == 1:
                            v.wait_ge(pe["U"], nth("U", i))
                        v.bn_stats(bn[:, b, tt, :], up(i, tt)).then_inc(dve_link, 1)
                    link[0] += TT
                    for tt in range(TT):
                        v.wait_ge(dve_link, link[0])
                        v.bn_aggr(mv[:, n, b, tt, :], bn[:, b, tt, :]).then_inc(dve_var, 1)
                    v.wait_ge(dve_var, TT * nth("U", i))
                    v.tensor_scalar(veps[:, n, b, :], mv[:, n, b, :, 1], LN_EPS, None, ALU.add)\
                        .then_inc(dve["U"], 1)
                    if l == 3 and wide(i):
                        v.wait_ge(s_gb[b % 2], 16 * (b // 2 + 2))
                        for tt in range(TT):
                            v.scalar_tensor_tensor(out=res[:, b, tt, :], in0=up(i, tt), scalar=mv[:, n, b, tt, 0:1],
                                                   in1=gb[:, b % 2, 0, :], op0=ALU.subtract, op1=ALU.mult)\
                                .then_inc(dve["centred"], 1)
                elif kind == "N":
                    l, b = i
                    n = li[l]
                    v.wait_ge(pool_rstd, nth("U", i))
                    v.scalar_tensor_tensor(out=nmr[:, n, b, :], in0=mv[:, n, b, :, 0], scalar=-1.0,
                                           in1=rstd[:, n, b, :], op0=ALU.mult, op1=ALU.mult).then_inc(dve["N"], 1)
                    if wide(i):
                        k = nth("N", i)
                        v.wait_ge(pe["T"], k - 2)
                        v.tensor_scalar(yn[:, k % 2, 1, :], up(i, 1), mv[:, n, b, 1, 0:1], rstd[:, n, b, 1:2],
                                        ALU.subtract, ALU.mult).then_inc(dve["wide_rows"], 1)
                elif kind == "T":
                    l, b = i
                    k = nth("T", i)
                    if l == 0 and b >= 2:
                        v.wait_ge(pe["S"], nth("S", b - 2))
                        v.wait_ge(pe["V"], nth("V", b - 2))
                    if l == 2 and b < 2:
                        v.wait_ge(pe["S"], nth("S", b + 2))
                        v.wait_ge(pe["V"], nth("V", b + 2))
                    if l == 2 and b >= 2:
                        v.wait_ge(pe["U"], nth("U", (3, b - 2)))
                    for kf in range(KF):
                        done = KF * (k - 1) + kf
                        v.wait_ge(act["T"], done + 1)
                        v.tensor_copy(xmid[:, HI, b % 2, kf, :], layer_out(l, b)[:, kf, :]).then_inc(dve["T"], 1)
                        v.wait_ge(dve["T"], 2 * done + 1)
                        v.tensor_tensor(xmid[:, LO, b % 2, kf, :], layer_out(l, b)[:, kf, :],
                                        xmid[:, HI, b % 2, kf, :].bitcast(F32), ALU.subtract).then_inc(dve["T"], 1)
                elif kind in ("MN", "Y", "V", "PT"):
                    v.wait_ge(act[kind], nth(kind, i))
                    v.tensor_tensor(pair(kind, i, LO), bank(kind, i), pair(kind, i, HI).bitcast(F32),
                                    ALU.subtract).then_inc(dve[kind], 1)
                elif kind == "ROWS":
                    if i == 0:
                        selectors()
                    bias_rows(i)
                elif kind == "CB":
                    cms_biases()
                elif kind == "S":
                    v.wait_ge(pe["S"], nth("S", i))
                    step(v.tensor_reduce(smax[:, i, :], bank("S", i), AX_X, ALU.max))
                    v.tensor_scalar(nmax[:, i, :], smax[:, i, :], -V ** -0.5, None, ALU.mult).then_inc(dve["max"], 1)
                elif kind == "E":
                    v.wait_ge(act["E"], TT * nth("E", i))
                    step(v.reciprocal(rsum[:, i, :], ssum[:, i, :]))
                    for tt in range(TT):
                        v.tensor_scalar(prob[:, tt, :], prob[:, tt, :], rsum[:, i, tt:tt + 1], None, ALU.mult)\
                            .then_inc(dve["E"], 1)
                elif kind == "A":
                    v.wait_ge(act["A"], KF * nth("A", i))
                    for kf in range(KF):
                        v.scalar_tensor_tensor(out=attn_of(i, LO, kf), in0=bank("A", i)[:, kf, :],
                                               scalar=sv[:, BP + kf:BP + kf + 1], in1=attn_of(i, HI, kf).bitcast(F32),
                                               op0=ALU.add, op1=ALU.subtract).then_inc(dve["A"], 1)
                elif kind in ("H1", "H2B"):
                    m = hid(0 if kind == "H1" else 1, *i)
                    v.wait_ge(act["hidden"], 2 * (m + 1))
                    v.tensor_tensor(hidden[:, m % HID_SLOTS, LO, :], hidden_full[:, m % 2, :],
                                    hidden[:, m % HID_SLOTS, HI, :].bitcast(F32), ALU.subtract)\
                        .then_inc(dve["hidden"], 1)
                elif kind == "CE":
                    n = 0
                    for kf in range(KF):
                        n += CB
                        v.wait_ge(act["CE"], CB * KF * i + n)
                        for j in range(CB):
                            b = CB * i + j
                            v.scalar_tensor_tensor(out=cms[:, LO, kf, j * S:(j + 1) * S],
                                                   in0=acc[:, kf, j * S:(j + 1) * S], scalar=cbias[:, kf, b:b + 1],
                                                   in1=cms[:, HI, kf, j * S:(j + 1) * S].bitcast(F32),
                                                   op0=ALU.add, op1=ALU.subtract).then_inc(dve["CE"], 1)
                    for j in range(CB):
                        for kf in range(KF):
                            b = CB * i + j
                            v.scalar_tensor_tensor(out=res[:, b, kf, :], in0=acc[:, kf, j * S:(j + 1) * S],
                                                   scalar=rbias[:, kf, b:b + 1], in1=res[:, b, kf, :],
                                                   op0=ALU.add, op1=ALU.add).then_inc(dve["CE"], 1)
                elif kind == "Z":
                    b, kf = i
                    c, j = b // CB, b % CB
                    if c < NC - 1:
                        v.wait_ge(pe["hidden_used"], hid(1, c, HT - 1) + 1)
                    else:
                        v.wait_ge(pe["end"], kf + 1)
                    v.wait_ge(dve["CE"], 2 * CB * KF * (c + 1))
                    v.tensor_tensor(res[:, b, kf, :], acc[:, kf, j * S:(j + 1) * S], res[:, b, kf, :], ALU.add)\
                        .then_inc(dve["z"], 1)
                elif kind == "ME":
                    b, kf = i
                    z = res[:, b, kf, :]
                    v.wait_ge(dve["z"], nth("Z", i))
                    if b >= 2:
                        v.wait_ge(pe["U"], nth("U", (2, b - 2)))
                    v.tensor_scalar(xin[:, HI, b % 2, kf, :], z, 0.0, 1.0, ALU.max, ALU.min).then_inc(dve["ME"], 1)
                    v.tensor_scalar(z, z, 0.0, 1.0, ALU.max, ALU.min).then_inc(dve["ME"], 1)
                    if b % 2 == 0:
                        v.wait_ge(dve["ME"], me_count(b, kf))
                        v.tensor_tensor(xin[:, LO, b % 2, kf, :], z, xin[:, HI, b % 2, kf, :].bitcast(F32),
                                        ALU.subtract).then_inc(dve_me_lo, 1)
                elif kind == "F":
                    l, b = i
                    n = li[l]
                    k = nth("F", i)
                    v.wait_ge(pool_rstd, nth("U", i))
                    v.wait_ge(s_gb[b % 2], 16 * (b // 2 + 2))
                    for tt in range(TT):
                        if wide(i):
                            v.wait_ge(dve["centred"], TT * (b - B + CB) + tt + 1)
                        else:
                            step(v.scalar_tensor_tensor(out=res[:, b, tt, :], in0=up(i, tt),
                                                        scalar=mv[:, n, b, tt, 0:1], in1=gb[:, b % 2, 0, :],
                                                        op0=ALU.subtract, op1=ALU.mult))
                        v.scalar_tensor_tensor(out=res[:, b, tt, :], in0=res[:, b, tt, :],
                                               scalar=rstd[:, n, b, tt:tt + 1], in1=gb[:, b % 2, 1, :],
                                               op0=ALU.mult, op1=ALU.add).then_inc(dve["F"], 1)

        @block.tensor
        def _(t):
            def take(step):
                if before[step]:
                    for s, n in freed(before[step]):
                        t.wait_ge(s, n)

            def products(out, pairs):
                todo = [(lhs(p), rhs(q)) for lhs, rhs in pairs for p, q in PASSES]
                for n, (l, r) in enumerate(todo):
                    ins = t.matmul(out, l, r, start=(n == 0), stop=(n == len(todo) - 1))
                return ins

            for kind, i in ORDER:
                if (kind, i, 0) in bank_of:
                    take((kind, i, 0))
                if kind == "WARM":
                    if nth("WARM", i) == 1:
                        t.wait_ge(pool_zero, 2)
                    for _ in range(i[1]):
                        t.matmul(ring[bank_of[(kind, i, 0)]][:, :], hidden[:, 0, HI, 0:P], hidden[:, 0, HI, :],
                                 start=True, stop=True)
                elif kind == "D":
                    l, b = i
                    t.wait_ge(*split_done(("adp", i)))
                    if l == 0:
                        t.wait_ge(*split_done(("x", b)))
                    elif l == 2:
                        t.wait_ge((dve_me_lo, pool_me)[b % 2], KF * (b // 2 + 1))
                    else:
                        t.wait_ge(dve["T"], 2 * KF * nth("T", (2, b)))
                    products(bank("D", i)[:, 0, :],
                             [(lambda p, kf=kf: adp[:, p, adp_slot[i], kf * P:(kf + 1) * P],
                               lambda p, kf=kf: layer_in(l, b, p)[:, kf, :]) for kf in range(KF)])\
                        .then_inc(pe["D"], 1)
                elif kind == "U":
                    l, b = i
                    k = nth("D", i)
                    t.wait_ge(dve_rows, b + 1)
                    for tt in range(TT):
                        if wide(i) and tt == 1:
                            take(("U", i, tt))
                        o = up(i, tt)
                        t.matmul(o, ones_row[:, li[l], :], rows[:, b, :], start=True, stop=False)
                        for p in (HI, LO):
                            for kf in range(KF):
                                t.matmul(o[:, kf * P:(kf + 1) * P], layer_in(l, b, p)[:, kf, tt * P:(tt + 1) * P],
                                         ident_r[:, :], start=False, stop=False)
                        if tt == 0:
                            t.wait_ge(dve["D"], k)
                        for n, (p, q) in enumerate(PASSES):
                            ins = t.matmul(o, act_h[:, k % 2, p, tt * P:(tt + 1) * P],
                                           adp[:, q, adp_slot[i], KF * P:KF * P + V],
                                           start=False, stop=(n == len(PASSES) - 1))
                        if wide(i) and tt == 0:
                            ins.then_inc(pe["U0"], 1)
                    ins.then_inc(pe["U"], 1)
                elif kind == "T":
                    k = nth("N", i)
                    for tt in range(TT):
                        t.wait_ge(*rows_done(i, tt))
                        for kf in range(KF):
                            ins = t.transpose(bank("T", i)[:, kf, tt * P:(tt + 1) * P],
                                              yn[:, k % 2, tt, kf * P:(kf + 1) * P], ident)
                    ins.then_inc(pe["T"], 1)
                elif kind == "MN":
                    for j in (2 * i, 2 * i + 1):
                        t.wait_ge(*split_done(("mn", j)))
                    for it in range(KF):
                        ins = products(bank("MN", i)[:, it, :],
                                       [(lambda p, kd=kd: w4[:, p, 4 * i + kd, it * P:(it + 1) * P],
                                         lambda p, kd=kd: w4[:, p, 4 * i + 2 + kd, :]) for kd in range(KF)])
                    ins.then_inc(pe["MN"], 1)
                elif kind == "Y":
                    b = i
                    t.wait_ge(dve["T"], 2 * KF * nth("T", (0, b)))
                    t.wait_ge(dve["MN"], 1)
                    for jt in range(KF):
                        ins = products(bank("Y", i)[:, jt, :],
                                       [(lambda p, kf=kf: mn[:, p, 0, kf, jt * P:(jt + 1) * P],
                                         lambda p, kf=kf: xmid[:, p, b % 2, kf, :]) for kf in range(KF)])
                    ins.then_inc(pe["Y"], 1)
                elif kind == "V":
                    b = i
                    t.wait_ge(dve["MN"], 2)
                    for tt in range(TT):
                        ins = products(bank("V", i)[:, tt, :],
                                       [(lambda p, kf=kf: xmid[:, p, b % 2, kf, tt * P:(tt + 1) * P],
                                         lambda p, kf=kf: mn[:, p, 1, kf, :]) for kf in range(KF)])
                    ins.then_inc(pe["V"], 1)
                elif kind == "S":
                    b = i
                    t.wait_ge(dve["Y"], nth("Y", i))
                    for tt in range(TT):
                        ins = products(bank("S", i)[:, tt, :],
                                       [(lambda p, kf=kf: qk[:, p, kf, tt * P:(tt + 1) * P],
                                         lambda p, kf=kf: xmid[:, p, b % 2, kf, :]) for kf in range(KF)])
                    ins.then_inc(pe["S"], 1)
                elif kind == "PT":
                    t.wait_ge(dve["E"], TT * nth("E", i))
                    for ts in range(TT):
                        for tt in range(TT):
                            ins = t.transpose(bank("PT", i)[:, ts, tt * P:(tt + 1) * P],
                                              prob[:, tt, ts * P:(ts + 1) * P], ident)
                    ins.then_inc(pe["PT"], 1)
                elif kind == "A":
                    b = i
                    t.wait_ge(dve["PT"], nth("PT", i))
                    t.wait_ge(dve["V"], nth("V", i))
                    for jt in range(KF):
                        ins = products(bank("A", i)[:, jt, :],
                                       [(lambda p, ts=ts: vv[:, p, b % 2, ts, jt * P:(jt + 1) * P],
                                         lambda p, ts=ts: probT[:, p, ts, :]) for ts in range(TT)])
                    ins.then_inc(pe["A"], 1)
                elif kind == "H1":
                    c, ht = i
                    t.wait_ge(*split_done(("w", ht // 2)))
                    if ht == 0:
                        t.wait_ge(dve["A"], KF * nth("A", CB * c + CB - 1))
                    products(ring[bank_of[(kind, i, 0)]][:, :],
                             [(lambda p, kf=kf: w1[:, p, ht, kf, :],
                               lambda p, kf=kf: attn[:, c, p, kf, :]) for kf in range(KF)])\
                        .then_inc(pe["hidden"], 1)
                elif kind == "H2A":
                    c, ht = i
                    t.wait_ge(*split_done(("w", 8 + ht)))
                    o = ring[bank_of[(kind, i, 0)]][:, :]
                    n = 0
                    for kf in range(KF):
                        for p, q in PASSES:
                            t.matmul(o, w3[:, p, ht, kf, :], attn[:, c, q, kf, :], start=(n == 0), stop=False)
                            n += 1
                elif kind == "H2B":
                    c, ht = i
                    if ht == 0:
                        t.wait_ge(dve["CE"], 2 * CB * KF * c + CB * KF)
                    o = ring[bank_of[("H2A", i, 0)]][:, :]
                    n = 0
                    for kf in range(KF):
                        for p, q in PASSES:
                            ins = t.matmul(o, w3[:, p, ht, KF + kf, :], cms[:, q, kf, :], start=False,
                                           stop=(n == KF * len(PASSES) - 1))
                            n += 1
                    ins.then_inc(pe["hidden"], 1)
                elif kind == "END":
                    for ht in (HT - 2, HT - 1):
                        m = hid(1, NC - 1, ht)
                        t.wait_ge(dve["hidden"], m + 1)
                        for n, (p, q) in enumerate(PASSES):
                            ins = t.matmul(acc[:, i, :], w4[:, p, ht, i * P:(i + 1) * P],
                                           hidden[:, m % HID_SLOTS, q, :], start=False,
                                           stop=(ht == HT - 1 and n == len(PASSES) - 1))
                    ins.then_inc(pe["end"], 1)
                elif kind in ("CMS", "MOD"):
                    c, ht = i
                    phase = 0 if kind == "CMS" else 1
                    w, m = (w4 if phase else w2), hid(phase, c, ht)
                    t.wait_ge(*split_done(("w", (16 if phase else 4) + ht // 2)))
                    t.wait_ge(dve["hidden"], m + 1)
                    if ht == 0 and phase == 1:
                        t.wait_ge(dve["CE"], 2 * CB * KF * (c + 1))
                    if ht == 0 and phase == 0 and c >= 1:
                        t.wait_ge(dve["z"], CB * KF * c)
                    for ft in range(KF):
                        for n, (p, q) in enumerate(PASSES):
                            ins = t.matmul(acc[:, ft, :], w[:, p, ht, ft * P:(ft + 1) * P],
                                           hidden[:, m % HID_SLOTS, q, :], start=(ht == 0 and n == 0),
                                           stop=(ht == HT - 1 and n == len(PASSES) - 1))
                    ins.then_inc(pe["hidden_used"], 1)



def kernel(**inputs):
    import numpy as np
    import concourse.bacc as bacc
    from concourse.bass_utils import run_bass_kernel_spmd as run

    a = {k: np.asarray(v) for k, v in inputs.items()}
    out_shape = a["x"].shape

    def tiles(w):
        return w.reshape(w.shape[0] // P, P, w.shape[1]).transpose(1, 0, 2)

    def columns(*vecs):
        return np.concatenate([u.reshape(-1, P).T for u in vecs], axis=1)

    def cut(w):
        return w.reshape(P, -1, PIECE).transpose(1, 0, 2)

    def hidden_tiles(w):
        k, h = w.shape
        return w.reshape(k // P, P, h // P, P).transpose(1, 2, 0, 3).reshape(P, -1)

    weights = np.concatenate([
        np.stack([tiles(a["L1_cond_" + n].T if n != "Wp" else a["L1_cond_Wp"]).reshape(P, PIECE)
                  for n in ("Wq", "Wk", "Wv", "Wp")]),
        cut(hidden_tiles(a["L1_cond_cW1"])), cut(tiles(a["L1_cond_cW2"]).reshape(P, -1)),
        cut(hidden_tiles(a["L1_cond_mW1"])), cut(tiles(a["L1_cond_mW2"]).reshape(P, -1))])
    adapters = np.stack([
        np.concatenate([tiles(a[f"L{l}_cond_W_down"][e]).reshape(P, -1), a[f"L{l}_cond_W_up"][e]], axis=1)
        for l in LAYERS for e in range(E)])
    adapters0 = np.stack([np.concatenate([adapters[e], columns(
        a["L0_cond_b_down"][e], a["L0_cond_gamma"][e], a["L0_cond_beta"][e],
        a["L2_cond_b_down"][e], a["L2_cond_ln_w"][e], a["L2_cond_ln_b"][e],
        a["L3_cond_b_down"][e])], axis=1) for e in range(E)])
    expert_rows = np.concatenate([a["L0_cond_b_up"], a["L2_cond_b_up"], a["L3_cond_b_up"],
                                  a["L3_cond_gamma"], a["L3_cond_beta"]], axis=1)
    vecs = columns(*(a["L1_cond_" + n] for n in ("cb1", "mb1", "bp", "cb2", "mb2")))
    xs = a["x"].transpose(0, 2, 1).reshape(B, KF, P, S).transpose(0, 2, 1, 3).reshape(B, P, KF * S)
    arrays = {
        "roles": a["itok_B_1_2"].reshape(1, B), "codes": a["itok_B_17_1546"].reshape(1, B),
        "xs": xs, "weights": weights, "adapters0": adapters0, "adapters": adapters[E:],
        "expert_rows": expert_rows, "vecs": vecs}
    arrays = {f"in_{k}": np.ascontiguousarray(v) for k, v in arrays.items()}

    nc = bacc.Bacc("TRN2", target_bir_lowering=False, num_devices=1, dynamic_dma_scratch_size=1024)
    args = [nc.dram_tensor(k, v.shape, mybir.dt.from_np(v.dtype), kind="ExternalInput").ap()
            for k, v in arrays.items()]
    out = nc.dram_tensor("out_x", out_shape, F32, kind="ExternalOutput").ap()
    build(nc, *args, out)
    r = run(nc, [arrays], core_ids=[0])
    return r.results[0]["out_x"]
```
